# Optimizing a Trainium2 kernel written in Bass

```python
import numpy as np
import jax
import jax.numpy as jnp

def _softmax(x, axis=-1):
    return jax.nn.softmax(x, axis=axis)

def _gelu(x):
    return jax.nn.gelu(x, approximate=True)

def _silu(x):
    return jax.nn.silu(x)

def _sigmoid(x):
    return jax.nn.sigmoid(x)

def _layernorm(x, axis=-1, eps=1e-05):
    m = jnp.mean(x, axis=axis, keepdims=True)
    v = jnp.var(x, axis=axis, keepdims=True)
    return (x - m) / jnp.sqrt(v + eps)

def _scatter_add(tgt, idx, src, axis=0):
    return tgt.at[idx].add(src)

def _segment_sum(src, seg, n):
    return jax.ops.segment_sum(src, seg, n)
kernel_name = 'mk_adj_preln_d4_adj_r2_586047'

def setup_inputs(seed: int=0):
    np.random.seed(seed)
    _w = jnp.asarray

    def _rec_inputs():
        import jax
        import jax.numpy as jnp
        _gk = jax.random.key(seed)
        x = -5.207e-06 + 0.01001 * jax.random.normal(jax.random.fold_in(_gk, 1), (4096, 128), jnp.float32)
        _w = (1.0 + jnp.arange(4096, dtype=jnp.float32)) ** (-0.5)
        _w = _w / _w.mean()
        _pij = jnp.clip(0.000976562 * _w[:, None] * _w[None, :], 0.0, 1.0)
        _a = jax.random.uniform(jax.random.fold_in(_gk, 2), (4096, 4096)) < _pij
        _a = jnp.logical_or(_a, jnp.eye(4096, dtype=bool))
        _af = _a.astype(jnp.float32)
        _af = _af / jnp.maximum(_af.sum(-1, keepdims=True), 1.0)
        adj = _af
        return (x, adj)
    x, adj = _rec_inputs()

    def _L0_gnn_setup():
        import jax, jax.numpy as jnp
        import numpy as np
        MIN_NORM = 1e-15
        BALL_EPS = 0.004
        C_IN = 1.0
        C_OUT = 1.0

        def _norm(x):
            return jnp.clip(jnp.linalg.norm(x, axis=-1, keepdims=True), MIN_NORM, None)

        def artanh(x):
            return jnp.arctanh(jnp.clip(x, -1.0 + 1e-07, 1.0 - 1e-07))

        def proj(x, c):
            norm = _norm(x)
            maxnorm = (1.0 - BALL_EPS) / jnp.sqrt(c)
            return jnp.where(norm > maxnorm, x / norm * maxnorm, x)

        def expmap0(u, c):
            sc = jnp.sqrt(c)
            un = _norm(u)
            return jnp.tanh(sc * un) * u / (sc * un)

        def logmap0(p, c):
            sc = jnp.sqrt(c)
            pn = _norm(p)
            return artanh(sc * pn) * p / (sc * pn)

        def mobius_add(x, y, c):
            x2 = jnp.sum(x * x, -1, keepdims=True)
            y2 = jnp.sum(y * y, -1, keepdims=True)
            xy = jnp.sum(x * y, -1, keepdims=True)
            num = (1 + 2 * c * xy + c * y2) * x + (1 - c * x2) * y
            denom = 1 + 2 * c * xy + c * c * x2 * y2
            return num / jnp.clip(denom, MIN_NORM, None)

        def mobius_matvec(m, x, c):
            sc = jnp.sqrt(c)
            xn = _norm(x)
            mx = x @ m.T
            mxn = _norm(mx)
            res = jnp.tanh(mxn / xn * artanh(sc * xn)) * mx / (mxn * sc)
            zero_rows = jnp.all(mx == 0, axis=-1, keepdims=True)
            return jnp.where(zero_rows, jnp.zeros_like(res), res)
        key = jax.random.key(seed)
        k1, k2, k3, k4 = jax.random.split(key, 4)
        N, din, dout = (8192, 128, 128)
        x = jax.random.normal(k1, (N, din), dtype=jnp.float32) * 0.01
        adj = jax.random.uniform(k2, (N, N), dtype=jnp.float32)
        adj = adj / jnp.sum(adj, axis=-1, keepdims=True)
        bound = math_bound = float(np.sqrt(2.0) * np.sqrt(6.0 / (din + dout)))
        weight = jax.random.uniform(k3, (dout, din), dtype=jnp.float32, minval=-bound, maxval=bound)
        bias = jax.random.normal(k4, (dout,), dtype=jnp.float32) * 0.01
        return {'x': x, 'adj': adj, 'weight': weight, 'bias': bias}
    _L0_gnn_all = _L0_gnn_setup()
    _L0_gnn_in = {k: v for k, v in _L0_gnn_all.items() if k in ('weight', 'bias')}
    del _L0_gnn_all

    def _L1_gnn_setup():
        import jax, jax.numpy as jnp
        import numpy as np
        N = 8192
        U = 128
        AVG_DEGREE = 32
        key = jax.random.key(seed)
        kx, ka, kw = jax.random.split(key, 3)
        x = jax.random.normal(kx, (N, U), dtype=jnp.float32)
        adj = (jax.random.uniform(ka, (N, N)) < AVG_DEGREE / N).astype(jnp.float32)
        W = jax.random.normal(kw, (U, U), dtype=jnp.float32) * 0.05
        b = jnp.zeros((U,), dtype=jnp.float32)
        return {'x': x, 'adj': adj, 'W': W, 'b': b}
    _L1_gnn_all = _L1_gnn_setup()
    _L1_gnn_in = {k: v for k, v in _L1_gnn_all.items() if k in ('W', 'b')}
    del _L1_gnn_all

    def _L2_gnn_setup():
        import jax, jax.numpy as jnp
        import numpy as np
        N = 8192
        IN_DIM = 128
        OUT_DIM = 128

        def _message(X, A, W):
            deg = jnp.sum(A, axis=1, keepdims=True)
            A_norm = A / jnp.where(deg > 0, deg, 1.0)
            return A_norm @ X @ W
        key = jax.random.key(seed)
        k1, k2, k3, k4 = jax.random.split(key, 4)
        X = jax.random.normal(k1, (N, IN_DIM), dtype=jnp.float32)
        A = jax.random.uniform(k2, (N, N), dtype=jnp.float32)
        W_in = jax.random.normal(k3, (IN_DIM, OUT_DIM), dtype=jnp.float32) / np.sqrt(IN_DIM)
        W_out = jax.random.normal(k4, (IN_DIM, OUT_DIM), dtype=jnp.float32) / np.sqrt(IN_DIM)
        return {'X': X, 'A': A, 'W_in': W_in, 'W_out': W_out}
    _L2_gnn_all = _L2_gnn_setup()
    _L2_gnn_in = {k: v for k, v in _L2_gnn_all.items() if k in ('W_in', 'W_out')}
    del _L2_gnn_all

    def _L3_gnn_setup():
        import jax, jax.numpy as jnp
        import numpy as np

        def _lap_mul(A, x):
            d = 1.0 / jnp.sqrt(jnp.sum(A, axis=-1))
            return d[:, None] * (A @ (d[:, None] * x))
        key = jax.random.key(seed)
        k1, k2, k3, k4, k5, k6 = jax.random.split(key, 6)
        N, D_IN, D_OUT = (2048, 128, 128)
        x = jax.random.normal(k1, (N, D_IN), dtype=jnp.float32)
        A = jax.random.uniform(k2, (N, N), dtype=jnp.float32)
        s1 = 1.0 / np.sqrt(D_IN)
        W1 = jax.random.uniform(k3, (D_IN, D_OUT), minval=-s1, maxval=s1, dtype=jnp.float32)
        b1 = jax.random.uniform(k4, (D_OUT,), minval=-s1, maxval=s1, dtype=jnp.float32)
        W2 = jax.random.uniform(k5, (D_IN, D_OUT), minval=-s1, maxval=s1, dtype=jnp.float32)
        b2 = jax.random.uniform(k6, (D_OUT,), minval=-s1, maxval=s1, dtype=jnp.float32)
        return {'x': x, 'A': A, 'W1': W1, 'b1': b1, 'W2': W2, 'b2': b2, 'sigma': 1, 'k': 4}
    _L3_gnn_all = _L3_gnn_setup()
    _L3_gnn_in = {k: v for k, v in _L3_gnn_all.items() if k in ('W1', 'b1', 'W2', 'b2')}
    del _L3_gnn_all
    return {'x': x, 'adj': adj, 'L0_gnn_weight': _L0_gnn_in['weight'], 'L0_gnn_bias': _L0_gnn_in['bias'], 'L1_gnn_W': _L1_gnn_in['W'], 'L1_gnn_b': _L1_gnn_in['b'], 'L2_gnn_W_in': _L2_gnn_in['W_in'], 'L2_gnn_W_out': _L2_gnn_in['W_out'], 'L3_gnn_W1': _L3_gnn_in['W1'], 'L3_gnn_b1': _L3_gnn_in['b1'], 'L3_gnn_W2': _L3_gnn_in['W2'], 'L3_gnn_b2': _L3_gnn_in['b2']}

def reference(x, adj, L0_gnn_weight, L0_gnn_bias, L1_gnn_W, L1_gnn_b, L2_gnn_W_in, L2_gnn_W_out, L3_gnn_W1, L3_gnn_b1, L3_gnn_W2, L3_gnn_b2):
    import jax
    import jax.numpy as jnp

    def _L0_gnn_ref(x, adj, weight, bias):
        import jax, jax.numpy as jnp
        import numpy as np
        MIN_NORM = 1e-15
        BALL_EPS = 0.004
        C_IN = 1.0
        C_OUT = 1.0

        def _norm(x):
            return jnp.clip(jnp.linalg.norm(x, axis=-1, keepdims=True), MIN_NORM, None)

        def artanh(x):
            return jnp.arctanh(jnp.clip(x, -1.0 + 1e-07, 1.0 - 1e-07))

        def proj(x, c):
            norm = _norm(x)
            maxnorm = (1.0 - BALL_EPS) / jnp.sqrt(c)
            return jnp.where(norm > maxnorm, x / norm * maxnorm, x)

        def expmap0(u, c):
            sc = jnp.sqrt(c)
            un = _norm(u)
            return jnp.tanh(sc * un) * u / (sc * un)

        def logmap0(p, c):
            sc = jnp.sqrt(c)
            pn = _norm(p)
            return artanh(sc * pn) * p / (sc * pn)

        def mobius_add(x, y, c):
            x2 = jnp.sum(x * x, -1, keepdims=True)
            y2 = jnp.sum(y * y, -1, keepdims=True)
            xy = jnp.sum(x * y, -1, keepdims=True)
            num = (1 + 2 * c * xy + c * y2) * x + (1 - c * x2) * y
            denom = 1 + 2 * c * xy + c * c * x2 * y2
            return num / jnp.clip(denom, MIN_NORM, None)

        def mobius_matvec(m, x, c):
            sc = jnp.sqrt(c)
            xn = _norm(x)
            mx = x @ m.T
            mxn = _norm(mx)
            res = jnp.tanh(mxn / xn * artanh(sc * xn)) * mx / (mxn * sc)
            zero_rows = jnp.all(mx == 0, axis=-1, keepdims=True)
            return jnp.where(zero_rows, jnp.zeros_like(res), res)
        mv = mobius_matvec(weight, x, C_IN)
        res = proj(mv, C_IN)
        hyp_bias = proj(expmap0(bias[None, :], C_IN), C_IN)
        h = proj(mobius_add(res, hyp_bias, C_IN), C_IN)
        xt = logmap0(h, C_IN)
        support_t = adj @ xt
        h = proj(expmap0(support_t, C_IN), C_IN)
        xt = jax.nn.relu(logmap0(h, C_IN))
        h = proj(expmap0(xt, C_OUT), C_OUT)
        return h

    def _L1_gnn_ref(x, adj, W, b):
        import jax, jax.numpy as jnp
        import numpy as np
        N = 8192
        U = 128
        AVG_DEGREE = 32
        adj = jax.lax.stop_gradient(adj)
        neigh1 = adj @ x
        x1 = jax.nn.swish(neigh1 @ W + b)
        neigh2 = adj @ x1
        x2 = jax.nn.swish(neigh2 @ W + b)
        return x2

    def _L2_gnn_ref(X, A, W_in, W_out):
        import jax, jax.numpy as jnp
        import numpy as np
        N = 8192
        IN_DIM = 128
        OUT_DIM = 128

        def _message(X, A, W):
            deg = jnp.sum(A, axis=1, keepdims=True)
            A_norm = A / jnp.where(deg > 0, deg, 1.0)
            return A_norm @ X @ W
        X_in = _message(X, A, W_in)
        X_out = _message(X, A.T, W_out)
        return X_in + X_out

    def _L3_gnn_ref(x, A, W1, b1, W2, b2, sigma, k):
        import jax, jax.numpy as jnp
        import numpy as np

        def _lap_mul(A, x):
            d = 1.0 / jnp.sqrt(jnp.sum(A, axis=-1))
            return d[:, None] * (A @ (d[:, None] * x))
        z = _lap_mul(A, x) @ W1 + b1
        z = jax.nn.leaky_relu(z, negative_slope=0.1)
        sq = jnp.sum(z * z, axis=-1)
        d2 = sq[:, None] + sq[None, :] - 2.0 * (z @ z.T)
        d2 = jnp.maximum(d2, 0.0)
        S = jnp.sqrt(d2 + 1e-10)
        S = jnp.exp(-S / (2.0 * sigma))
        order = jnp.argsort(-S, axis=-1)
        ranks = jnp.argsort(order, axis=-1)
        S = jnp.where(ranks < k, S, 0.0)
        A2 = S + A
        out = _lap_mul(A2, x) @ W2 + b2
        return out
    h = jnp.maximum(_layernorm(x, axis=-1), 0.0)
    x = x + _L0_gnn_ref(h, adj, L0_gnn_weight, L0_gnn_bias)
    h = jnp.maximum(_layernorm(x, axis=-1), 0.0)
    x = x + _L1_gnn_ref(h, adj, L1_gnn_W, L1_gnn_b)
    h = jnp.maximum(_layernorm(x, axis=-1), 0.0)
    x = x + _L2_gnn_ref(h, adj, L2_gnn_W_in, L2_gnn_W_out)
    h = jnp.maximum(_layernorm(x, axis=-1), 0.0)
    x = x + _L3_gnn_ref(h, adj, L3_gnn_W1, L3_gnn_b1, L3_gnn_W2, L3_gnn_b2, 1, 4)
    return x

_drawn_inputs = setup_inputs


def setup_inputs(seed=0):
    import zlib

    import numpy as np

    out = dict(_drawn_inputs(seed))
    spreads = {'L1_gnn_b': (0.0, 0.1)}
    factors = {}
    for name, (base, spread) in spreads.items():
        noise = np.random.default_rng([zlib.crc32(name.encode()), seed]).standard_normal(out[name].shape)
        drawn = base * np.exp(spread * noise) if base else spread * noise
        out[name] = jnp.asarray(drawn.astype(out[name].dtype))
    for name, factor in factors.items():
        out[name] = (out[name] * factor).astype(out[name].dtype)
    return out
```

```python
from contextlib import ExitStack

import numpy as np

import concourse.bass as bass
from concourse import mybir
from concourse.alu_op_type import AluOpType as ALU

F32 = mybir.dt.float32
F32R = mybir.dt.float32r
U32 = mybir.dt.uint32
ACT = mybir.ActivationFunctionType
AX_X = mybir.AxisListType.X

P = 128
N = 4096
NK = N // P
HALF = N // 2
HK = NK // 2
BANK = 512
GROUP = 4
NG = NK // GROUP
BODY = 8
PEELED = 16
LOOPS = (NK - PEELED) // BODY
RAW, HI, LO = 4, 4, 2
KEPT = 2
TOPK = 4

MIN_NORM = 1e-15
MAX_NORM = float(np.float32(1.0) - np.float32(0.004))
CLIP = float(np.float32(1.0 - 1e-7))
ARTANH_MAX_NORM = float(np.arctanh(MAX_NORM))
LN_EPS = 1e-5
DIST_EPS = 1e-10

SWEEPS = [("T", 0, 0, "ball"), ("T", 1, 0, "ball"),
          ("T", 0, 1, "swish"), ("T", 1, 1, "swish"),
          ("T", 0, 0, "swish_norm"), ("T", 1, 0, "swish_norm"),
          ("A", 0, 1, "columns"), ("A", 1, 1, "columns"),
          ("T", 0, 1, "rows"), ("T", 1, 1, "rows"),
          ("T", 0, 0, "embed"), ("T", 1, 0, "embed"),
          ("T", 0, 0, "last"), ("T", 1, 0, "last")]
NS = len(SWEEPS)
LAST = NS - 2
SUMMED = (0, 1, 6, 7)

KINDS = ["enter", "enter"] + [s[3] for s in SWEEPS]
WEIGHT = {"enter": "ball", "ball": "ident", "swish": "swish", "swish_norm": "swish", "columns": "out",
          "rows": "in", "embed": "embed", "last": "last"}

NORM_V = ["stats", "diff", "msum", "vsum", "dsq", "var", "vareps", "rstd", "shift", "normed"]
ARTANH_V = ["plus", "minus", "inv", "ratio", "sq", "p1", "p2", "p3", "p4", "small", "gap", "pick", "artanh"]

STEPS = {
    "enter": {
        "v": NORM_V + ["h_sum", "mx_sum", "mx_bias", "mb_sum", "floor", "h_clip"]
        + ["h_" + n for n in ARTANH_V]
        + ["hn_inv", "arg", "arg2", "cap", "mx_inv", "q", "q_sq", "x2", "xy", "xy1", "top", "left", "x2y2",
           "den", "den_floor", "den_inv", "top_q", "a", "c", "a_mx", "c_bias", "moved", "m_sum",
           "m_floor", "m_clip"] + ["m_" + n for n in ARTANH_V] + ["m_inv2", "m_scale", "out"],
        "a": ["std", "h", "hT", "h_sq", "mx_sq", "norms", "h_ln", "tanh", "m_sq", "m_norm", "m_ln"],
        "p": ["hT", "nat"]},
    "ball": {
        "v": ["s_sum", "s_floor", "s_inv", "s_scale", "u", "u_sum", "u_floor", "u_inv", "u_scale", "res"]
        + NORM_V,
        "a": ["yT", "s_sq", "s_norm", "u_sq", "u_norm", "u_tanh", "std", "out"], "p": ["nat"]},
    "swish": {"v": ["biased"], "a": ["yT", "out"], "p": ["nat"]},
    "swish_norm": {"v": ["biased", "res"] + NORM_V, "a": ["yT", "swish", "std", "out"], "p": ["nat"]},
    "columns": {"v": ["sum", "pos", "masked", "one", "safe", "inv", "res"], "a": ["yT"], "p": ["nat"]},
    "rows": {"v": ["sum", "pos", "masked", "one", "safe", "inv", "dinv", "res"] + NORM_V
             [:-1] + ["rstd_d", "shift_d", "normed"],
             "a": ["yT", "droot", "std", "out"], "p": ["nat"]},
    "embed": {"v": ["z", "leaky", "z_sum"], "a": ["yT", "z_sq"], "p": ["nat"]},
    "last": {"v": ["biased", "out"], "a": ["yT"], "p": ["near", "nat"]},
}
PSUM_READ = {"enter": ("v", "moved"), "ball": ("v", "u"), "swish": ("v", "biased"),
             "swish_norm": ("v", "biased"), "columns": ("v", "res"), "rows": ("v", "res"),
             "embed": ("v", "z"), "last": ("v", "out")}
OPERAND = {"enter": ("v", "out"), "ball": ("a", "out"), "swish": ("a", "out"),
           "swish_norm": ("a", "out"), "rows": ("a", "out")}
OPERAND_OF = {0: -2, 2: 0, 4: 2, 6: 4, 8: 4, 10: 8}

GV = ["neg", "eps", "sum", "total", "dlast", "scale", "operand", "places"]
GA = ["dist", "weight", "root"]
ZP = ["zT0", "zT1", "sq0", "sq1"]
ZA = ["hi0", "sq0", "hi1", "sq1", "row0", "row1"]
ZV = ["lo0", "lo1", "row0", "row1"]


def step_counts():
    at = {}
    for who in "vap":
        n = 0
        for e, kind in enumerate(KINDS):
            at[who, e, "begin"] = n
            for name in STEPS[kind][who]:
                n += 1
                at[who, e, name] = n
            at[who, e, "end"] = n
    return at


def graph_layers(nc, x, adj, adj_t, w_ball_t, b_ball, w_swish, b_swish, w_in, w_out, w_embed, b_embed,
                 w_last, b_last, eye, rows_dram, out):
    at = step_counts()

    first_ring, tile_at = [], {}
    n = 0
    for s, (mat, half, _, _) in enumerate(SWEEPS):
        kept = KEPT if mat == "T" else 0
        first_ring.append(n - kept)
        for t in range(kept, NK):
            tile_at[n] = NK * s + t
            n += 1

    with ExitStack() as ctx:
        def sb(name, shape, dt=F32):
            return ctx.enter_context(nc.sbuf_tensor(name, shape, dt))

        def sem(name):
            return ctx.enter_context(nc.semaphore(name))

        raw = sb("raw", [P, RAW, HALF])
        kept_tiles = sb("kept_tiles", [P, 2, KEPT, HALF])
        hi = sb("hi", [P, HI, HALF], F32R)
        lo = sb("lo", [P, LO, HALF], F32R)
        operand = [sb("operand0", [P, NK, P]), sb("operand1", [P, NK, P])]
        res = sb("res", [P, NK, P])
        work = sb("work", [P, 2, HALF])
        yT, scr = work[:, 0, :], work[:, 1, :]
        split_x = sb("split_x", [P, 2, GROUP, 2, P], F32R)
        weights = {n: sb("weight_" + n, [P, P]) for n in ("ident", "ball", "swish", "in", "out", "embed", "last")}
        bias = {n: sb("bias_" + n, [P, P]) for n in ("ball", "swish", "embed", "last")}
        ball_bias = sb("ball_bias", [P, P])
        bb = sb("bb", [P, 8])
        stats = sb("stats", [P, HK, 6])
        SMALL = 40
        sm = sb("sm", [P, SMALL, HK])
        col_part = sb("col_part", [P, 2, NK])
        row_part = sb("row_part", [P, 2, NK])
        deg, pos, one, inv_sum = (sb(n, [P, NK]) for n in ("deg", "pos", "one", "inv_sum"))
        droot, dinv = sb("droot", [P, NK]), sb("dinv", [P, NK])
        z_sq = sb("z_sq", [P, NK])
        neg_sq = sb("neg_sq", [P, NK])
        pick_half = sb("pick_half", [P, P])
        two_rows = sb("two_rows", [P, P], F32R)
        top = sb("top", [P, 2, GROUP, 8])
        top_at = sb("top_at", [P, 2, GROUP, 8], U32)
        near_at = sb("near_at", [P, NK, TOPK], U32)
        near_w = sb("near_w", [P, NK, TOPK])
        gd = sb("gd", [P, 2, GROUP, TOPK])
        gs = sb("gs", [P, 2, 3, GROUP])
        dlast = sb("dlast", [P, NK])
        z = operand[1]
        zT = hi[:, :, :].rearrange("p (a b) n -> p a (b n)", a=2)
        sq_row = lo[:, :, :].rearrange("p a n -> p (a n)")
        dist = [operand[1][:, :, :].rearrange("p k f -> p (k f)"),
                work[:, :, :].rearrange("p a n -> p (a n)")]
        near_rows = operand[1][:, 0:HK, :].rearrange("p (r t) f -> p r t f", t=TOPK)
        near_sum = operand[1][:, HK:NK, :]

        ps = ctx.enter_context(nc.psum_tensor("ps", [P, 8, BANK], F32))

        def by_tile(ap):
            return ap.rearrange("p (k f) -> p k f", f=P)

        def flat(ap):
            return ap.rearrange("p k f -> p (k f)")

        def acc(half):
            return flat(ps[:, 4 * half:4 * half + 4, :])

        def nat(half):
            return by_tile(acc(half))

        def half_of(buf, half):
            return buf[:, half * HK:(half + 1) * HK]

        def per_node(v):
            return v.unsqueeze(2).broadcast_to([P, HK, P])

        def per_feature(v):
            return v[:, :].unsqueeze(1).broadcast_to([P, HK, P])

        raw_in = [sem(f"raw_in{i}") for i in range(RAW)]
        kept_in = [[sem(f"kept_in{h}_{i}") for i in range(KEPT)] for h in range(2)]
        x_in = [sem("x_in0"), sem("x_in1")]
        const_in = sem("const_in")
        CONSTS = 11
        hi_ready = sem("hi_ready")
        lo_ready = sem("lo_ready")
        tile_done = sem("tile_done")
        sx_hi, sx_lo = sem("sx_hi"), sem("sx_lo")
        step = {"v": sem("v_step"), "a": sem("a_step"), "p": sem("p_step")}
        setup_v, setup_a, setup_g = sem("setup_v"), sem("setup_a"), sem("setup_g")
        zp, za, zv = sem("zp"), sem("za"), sem("zv")
        z_staged = sem("z_staged")
        zz_done = sem("zz_done")
        zz_out = sem("zz_out")
        ranked = sem("ranked")
        gv, ga = sem("gv"), sem("ga")
        rows_out = [sem("rows_out0"), sem("rows_out1")]
        fetched = [sem(f"fetched{i}") for i in range(GROUP)]
        near_done = sem("near_done")
        done_out = sem("done_out")
        waited = sem("waited")

        block = ctx.enter_context(nc.Block())

        def wait(eng, who, e, name):
            if at[who, e, name] > 0:
                eng.wait_ge(step[who], at[who, e, name])

        class Steps:

            def __init__(self, eng, who):
                self.eng, self.who, self.count = eng, who, 0

            def did(self, e, name, ins):
                assert at[self.who, e, name] == self.count + 1, (KINDS[e], name)
                self.count += 1
                ins.then_inc(step[self.who], 1)

            def own(self):
                self.eng.wait_ge(step[self.who], self.count)

        class Woven:

            def __init__(self, steps):
                self.steps, self.behind = steps, 0
                if steps is not None:
                    self.behind = next(steps, None)

            def after(self, t):
                while self.behind is not None and self.steps is not None and self.behind <= t:
                    self.behind = next(self.steps, None)

            def finish(self):
                self.after(NK)

        def apart(eng):
            eng.sem_inc(waited)

        def wait_operand(eng, s, half):
            if s >= LAST:
                eng.wait_ge(gv, len(GV) * NG)
                return
            e = OPERAND_OF[s - s % 2] + half + 2
            who, name = OPERAND[KINDS[e]]
            wait(eng, who, e, name)

        def hi_slot_free(eng, s, t, i=0):
            if NK * s + t >= HI:
                eng.wait_ge(tile_done, NK * s + t - HI + 1 + BODY * i)

        @block.sync
        def _(sp):
            sp.dma_start(res[:, 0:HK, :], x.rearrange("(k p) f -> p k f", p=P)[:, 0:HK, :]).then_inc(x_in[0], 16)
            for name, src in (("ident", eye), ("ball", w_ball_t), ("swish", w_swish), ("in", w_in),
                              ("out", w_out), ("embed", w_embed), ("last", w_last)):
                sp.dma_start(weights[name][:], src).then_inc(const_in, 16)
            for name, src in (("ball", b_ball), ("swish", b_swish), ("embed", b_embed), ("last", b_last)):
                sp.dma_start(bias[name][:], src.rearrange("(a f) -> a f", a=1).broadcast_to([P, P])
                             ).then_inc(const_in, 16)
            sp.dma_start(res[:, HK:NK, :], x.rearrange("(k p) f -> p k f", p=P)[:, HK:NK, :]).then_inc(x_in[1], 16)

            rows_view = rows_dram.rearrange("(k p) f -> p k f", p=P)

            def store_rows(g, i=0):
                sp.wait_ge(gv, len(GV) * g + GV.index("operand") + 1 + 2 * len(GV) * i)
                apart(sp)
                if g >= 2:
                    sp.wait_ge(rows_out[g % 2], 16 * (g // 2) + 16 * i)
                apart(sp)
                k = bass.ds(GROUP * g + 2 * GROUP * i, GROUP)
                sp.dma_start(rows_view[:, k, :], operand[0][:, k, :]).then_inc(rows_out[g % 2], 16)

            for s, (mat, half, _, _) in enumerate(SWEEPS):
                kept = KEPT if mat == "T" else 0
                src = {"T": adj_t, "A": adj}[mat]

                def load(t, i=0):
                    r = first_ring[s] + t
                    if r >= RAW:
                        before = tile_at[r - RAW] if t < PEELED else NK * s + t - RAW
                        sp.wait_ge(lo_ready, before + 1 + BODY * i)
                    sp.dma_start(raw[:, r % RAW, :],
                                 src[bass.ds((t + BODY * i) * P, P), half * HALF:(half + 1) * HALF]
                                 ).then_inc(raw_in[r % RAW], 16)

                if s == LAST:
                    for t in range(kept, kept + RAW):
                        load(t)
                    store_rows(0)
                    store_rows(1)
                    with sp.Fori(0, NG // 2 - 1) as i:
                        store_rows(2, i)
                        store_rows(3, i)
                    for t in range(kept + RAW, PEELED):
                        load(t)
                else:
                    for t in range(PEELED):
                        if t >= kept:
                            load(t)
                        elif s < 2:
                            sp.dma_start(kept_tiles[:, half, t, :], src[t * P:(t + 1) * P, half * HALF:(half + 1) * HALF]
                                         ).then_inc(kept_in[half][t], 16)
                with sp.Fori(0, LOOPS) as i:
                    for t in range(PEELED, PEELED + BODY):
                        load(t, i)

            for h in range(2):
                wait(sp, "v", NS + h, "out")
                sp.dma_start(out.rearrange("(k p) f -> p k f", p=P)[:, h * HK:(h + 1) * HK, :],
                             half_of(res, h)).then_inc(done_out, 16)
            sp.wait_ge(done_out, 32)

        @block.scalar
        def _(act):
            steps = Steps(act, "a")
            did = steps.did

            def v(i):
                return sm[:, i, :]

            def begin(e):
                for who in "vp":
                    wait(act, who, e, "begin")
                if e > 0:
                    steps.own()

            def normalise(e, dst, name, behind):
                wait(act, "v", e, "vareps")
                did(e, "std", nc.scalar.activation(v(6), v(5), ACT.Sqrt))
                yield behind
                wait(act, "v", e, "normed")
                did(e, name, nc.scalar.activation(dst, by_tile(scr), ACT.Relu))

            def epilogue(e):
                kind, half = KINDS[e], e % 2
                if kind == "enter":
                    yield 1
                    begin(e)
                    yield from normalise(e, by_tile(scr), "h", 3)
                    yield 6
                    wait(act, "p", e, "hT")
                    did(e, "hT", nc.scalar.copy(yT, acc(1)))
                    steps.own()
                    did(e, "h_sq", nc.scalar.activation(scr, scr, ACT.Square))
                    yield 8
                    wait(act, "v", e, "h_sum")
                    wait(act, "p", e, "nat")
                    did(e, "mx_sq", nc.scalar.activation(scr, acc(1), ACT.Square))
                    yield 9
                    wait(act, "v", e, "mx_sum")
                    did(e, "norms", nc.scalar.activation(sm[:, 11:13, :], sm[:, 9:11, :], ACT.Sqrt))
                    yield 10
                    wait(act, "v", e, "h_ratio")
                    did(e, "h_ln", nc.scalar.activation(v(19), v(18), ACT.Ln))
                    yield 11
                    wait(act, "v", e, "arg2")
                    did(e, "tanh", nc.scalar.activation(v(27), v(26), ACT.Tanh))
                    yield 14
                    wait(act, "v", e, "moved")
                    did(e, "m_sq", nc.scalar.activation(yT, scr, ACT.Square))
                    wait(act, "v", e, "m_sum")
                    did(e, "m_norm", nc.scalar.activation(v(11), v(9), ACT.Sqrt))
                    yield 15
                    wait(act, "v", e, "m_ratio")
                    did(e, "m_ln", nc.scalar.activation(v(19), v(18), ACT.Ln))
                    return
                yield 10 if kind == "last" else 2
                begin(e)
                act.wait_ge(tile_done, NK * (e - 1))
                if kind == "last":
                    wait(act, "p", e, "near")
                did(e, "yT", nc.scalar.copy(yT, acc(half)))
                if kind == "ball":
                    yield 5
                    wait(act, "p", e, "nat")
                    did(e, "s_sq", nc.scalar.activation(scr, acc(half), ACT.Square))
                    yield 6
                    wait(act, "v", e, "s_sum")
                    did(e, "s_norm", nc.scalar.activation(v(10), v(9), ACT.Sqrt))
                    yield 8
                    wait(act, "v", e, "u")
                    did(e, "u_sq", nc.scalar.activation(yT, scr, ACT.Square))
                    yield 9
                    wait(act, "v", e, "u_sum")
                    did(e, "u_norm", nc.scalar.activation(v(14), v(13), ACT.Sqrt))
                    wait(act, "v", e, "u_floor")
                    did(e, "u_tanh", nc.scalar.activation(v(16), v(15), ACT.Tanh))
                elif kind in ("swish", "swish_norm"):
                    yield 6
                    wait(act, "v", e, "biased")
                    if kind == "swish":
                        did(e, "out", nc.scalar.activation(half_of(operand[0], half), by_tile(scr), ACT.Silu))
                    else:
                        did(e, "swish", nc.scalar.activation(yT, scr, ACT.Silu))
                elif kind == "rows":
                    yield 6
                    wait(act, "v", e, "sum")
                    did(e, "droot", nc.scalar.activation(droot[:], deg[:], ACT.Sqrt))
                elif kind == "embed":
                    yield 7
                    wait(act, "v", e, "leaky")
                    did(e, "z_sq", nc.scalar.activation(by_tile(yT), half_of(z, half), ACT.Square))
                if kind in ("ball", "swish_norm", "rows"):
                    yield {"ball": 13, "swish_norm": 10, "rows": 11}[kind]
                    dst = operand[0 if kind == "rows" else 1]
                    yield from normalise(e, half_of(dst, half), "out", {"ball": 15, "swish_norm": 12, "rows": 13}[kind])

            act.wait_ge(const_in, 16 * CONSTS)
            nc.scalar.activation(ball_bias[:], bias["ball"][:], ACT.Square, accum_out=bb[:, 0:1]).then_inc(setup_a, 1)
            act.wait_ge(setup_a, 1)
            nc.scalar.activation(bb[:, 1:2], bb[:, 0:1], ACT.Sqrt).then_inc(setup_a, 1)
            act.wait_ge(setup_v, 1)
            nc.scalar.activation(bb[:, 3:4], bb[:, 2:3], ACT.Tanh).then_inc(setup_a, 1)
            act.wait_ge(setup_v, 4)
            nc.scalar.activation(scr[:, 0:P], ball_bias[:], ACT.Square, accum_out=bb[:, 6:7]).then_inc(setup_a, 1)
            act.wait_ge(setup_a, 4)

            for _ in epilogue(0):
                pass

            for s, (mat, half, src, kind) in enumerate(SWEEPS):
                kept = KEPT if mat == "T" else 0
                sums = {"T": col_part, "A": row_part}[mat]

                if s == LAST:
                    for _ in epilogue(s + 1):
                        pass
                    for h in range(2):
                        sq_buf = work[:, h, :]
                        act.wait_ge(zp, ZP.index(f"zT{h}") + 1)
                        if h == 0:
                            wait(act, "v", s + 1, "end")
                            act.wait_ge(tile_done, NK * s)
                        nc.scalar.copy(zT[:, 0, h * HALF:(h + 1) * HALF], acc(h)).then_inc(za, 1)
                        nc.scalar.activation(sq_buf, acc(h), ACT.Square).then_inc(za, 1)
                    for h in range(2):
                        act.wait_ge(zp, ZP.index(f"sq{h}") + 1)
                        nc.scalar.copy(sq_row[:, h * HALF:(h + 1) * HALF], acc(h)).then_inc(za, 1)

                    def weigh(g, i):
                        act.wait_ge(gv, len(GV) * g + GV.index("eps") + 1 + 2 * len(GV) * i)
                        nc.scalar.activation(gd[:, g % 2, :, :], gd[:, g % 2, :, :], ACT.Sqrt).then_inc(ga, 1)
                        act.wait_ge(ga, len(GA) * g + 1 + 2 * len(GA) * i)
                        k = bass.ds(GROUP * g + 2 * GROUP * i, GROUP)
                        nc.scalar.activation(near_w[:, k, :], gd[:, g % 2, :, :], ACT.Exp, scale=-0.5).then_inc(ga, 1)

                    def root(g, i):
                        act.wait_ge(gv, len(GV) * g + GV.index("total") + 1 + 2 * len(GV) * i)
                        nc.scalar.activation(gs[:, g % 2, 1, :], gs[:, g % 2, 0, :], ACT.Sqrt).then_inc(ga, 1)

                    def leave(g, i=0):
                        for r in range(GROUP):
                            k = GROUP * g + r
                            for c in range(4):
                                act.wait_ge(zz_done, 4 * k + c + 1 + 8 * GROUP * i)
                                if c == 0 and k >= 2:
                                    act.wait_ge(ranked, 2 * (k - 1) + 4 * GROUP * i)
                                apart(act)
                                nc.scalar.activation(dist[k % 2][:, c * 2 * BANK:(c + 1) * 2 * BANK],
                                                     ps[:, 2 * c:2 * c + 2, :].rearrange("p b n -> p (b n)"),
                                                     ACT.Identity, bias=neg_sq[:, bass.ds(k + 2 * GROUP * i, 1)],
                                                     scale=2.0).then_inc(zz_out, 1)
                            if g > 0 and r == 0:
                                weigh(g - 1, i)
                            if g > 0 and r == 2:
                                root(g - 1, i)

                    act.wait_ge(zv, len(ZV))
                    act.wait_ge(zp, len(ZP))
                    leave(0)
                    leave(1)
                    with act.Fori(0, NG // 2 - 1) as i:
                        leave(2, i)
                        leave(3, i)
                    weigh(NG - 1, 0)
                    root(NG - 1, 0)

                def split_group(g, i=0):
                    if g in (0, NG // 2):
                        wait_operand(act, s, g // (NG // 2))
                    if NG * s + g >= 2:
                        act.wait_ge(tile_done, NK * s + GROUP * (g - 1) + BODY * i)
                    nc.scalar.copy(split_x[:, g % 2, :, 0, :], operand[src][:, bass.ds(GROUP * g + BODY * i, GROUP), :]
                                   ).then_inc(sx_hi, 1)

                def hi_part(t, i=0):
                    r = first_ring[s] + t
                    if t < kept:
                        act.wait_ge(kept_in[half][t], 16)
                        tile = kept_tiles[:, half, t, :]
                    else:
                        act.wait_ge(raw_in[r % RAW], 16 * (r // RAW + 1) + 16 * (BODY // RAW) * i)
                        tile = raw[:, r % RAW, :]
                    hi_slot_free(act, s, t, i)
                    if s in SUMMED:
                        nc.scalar.activation(hi[:, t % HI, :], tile, ACT.Identity,
                                             accum_out=sums[:, half, bass.ds(t + BODY * i, 1)]).then_inc(hi_ready, 1)
                    else:
                        nc.scalar.copy(hi[:, t % HI, :], tile).then_inc(hi_ready, 1)

                if s == LAST:
                    act.wait_ge(zz_done, 4 * NK)
                epi = Woven(None if s == LAST else epilogue(s + 1))
                for t in range(PEELED):
                    if t % GROUP == 0:
                        split_group(t // GROUP)
                    hi_part(t)
                    epi.after(t)
                epi.finish()
                wait_operand(act, s, 1)
                with act.Fori(0, LOOPS) as i:
                    for t in range(PEELED, PEELED + BODY):
                        if t % GROUP == 0:
                            split_group(t // GROUP, i)
                        hi_part(t, i)
            for _ in epilogue(NS + 1):
                pass

        @block.vector
        def _(dve):
            steps = Steps(dve, "v")

            def v(i):
                return sm[:, i, :]

            def did(e, name, ins):
                steps.did(e, name, ins)
                steps.own()

            def row_sum(dst, src):
                return nc.vector.tensor_reduce(dst, src, AX_X, ALU.add)

            def begin(e):
                for who in "ap":
                    wait(dve, who, e, "begin")

            def norm_stats(e, half, behind):
                for k in range(HK):
                    ins = nc.vector.bn_stats(stats[:, k, :], res[:, half * HK + k, :])
                    if k == HK // 2 - 1:
                        yield behind
                did(e, "stats", ins)
                did(e, "diff", nc.vector.tensor_tensor(v(0), stats[:, :, 1], stats[:, :, 4], ALU.subtract))
                did(e, "msum", nc.vector.tensor_tensor(v(1), stats[:, :, 1], stats[:, :, 4], ALU.add))
                did(e, "vsum", nc.vector.tensor_tensor(v(2), stats[:, :, 2], stats[:, :, 5], ALU.add))
                did(e, "dsq", nc.vector.tensor_tensor(v(3), v(0), v(0), ALU.mult))
                did(e, "var", nc.vector.scalar_tensor_tensor(v(4), v(3), P / 4.0, v(2), ALU.mult, ALU.add))
                did(e, "vareps", nc.vector.tensor_scalar(v(5), v(4), 1.0 / P, LN_EPS, ALU.mult, ALU.add))
                yield behind + 2
                wait(dve, "a", e, "std")
                did(e, "rstd", nc.vector.reciprocal(v(7), v(6)))
                did(e, "shift", nc.vector.scalar_tensor_tensor(v(8), v(1), -0.5, v(7), ALU.mult, ALU.mult))
                if KINDS[e] == "rows":
                    did(e, "rstd_d", nc.vector.tensor_tensor(v(7), v(7), half_of(dinv, half), ALU.mult))
                    did(e, "shift_d", nc.vector.tensor_tensor(v(8), v(8), half_of(dinv, half), ALU.mult))
                for k in range(HK):
                    ins = nc.vector.tensor_scalar(by_tile(scr)[:, k, :], res[:, half * HK + k, :], sm[:, 7, k:k + 1],
                                                  sm[:, 8, k:k + 1], ALU.mult, ALU.add)
                did(e, "normed", ins)

            def artanh(e, pre, u, dst):
                did(e, pre + "plus", nc.vector.tensor_scalar(v(15), u, 1.0, None, ALU.add))
                did(e, pre + "minus", nc.vector.tensor_scalar(v(16), u, -1.0, 1.0, ALU.mult, ALU.add))
                did(e, pre + "inv", nc.vector.reciprocal(v(17), v(16)))
                did(e, pre + "ratio", nc.vector.tensor_tensor(v(18), v(15), v(17), ALU.mult))
                did(e, pre + "sq", nc.vector.tensor_tensor(v(20), u, u, ALU.mult))
                did(e, pre + "p1", nc.vector.tensor_scalar(v(21), v(20), 1.0 / 7, 1.0 / 5, ALU.mult, ALU.add))
                did(e, pre + "p2", nc.vector.tensor_tensor(v(21), v(21), v(20), ALU.mult))
                did(e, pre + "p3", nc.vector.scalar_tensor_tensor(v(21), v(21), 1.0 / 3, v(20), ALU.add, ALU.mult))
                did(e, pre + "p4", nc.vector.scalar_tensor_tensor(v(21), v(21), 1.0, u, ALU.add, ALU.mult))
                did(e, pre + "small", nc.vector.tensor_scalar(v(22), u, 0.1, None, ALU.is_lt))
                wait(dve, "a", e, pre + "ln")
                did(e, pre + "gap", nc.vector.scalar_tensor_tensor(v(23), v(19), -0.5, v(21), ALU.mult, ALU.add))
                did(e, pre + "pick", nc.vector.tensor_tensor(v(23), v(23), v(22), ALU.mult))
                did(e, pre + "artanh", nc.vector.scalar_tensor_tensor(dst, v(19), 0.5, v(23), ALU.mult, ALU.add))

            def enter(e, half):
                yield 0
                begin(e)
                dve.wait_ge(x_in[half], 16)
                yield from norm_stats(e, half, 1)
                yield 6
                wait(dve, "a", e, "h_sq")
                did(e, "h_sum", row_sum(v(9), by_tile(scr)))
                yield 8
                wait(dve, "a", e, "mx_sq")
                did(e, "mx_sum", row_sum(v(10), by_tile(scr)))
                yield 9
                did(e, "mx_bias", nc.vector.tensor_tensor(by_tile(scr), nat(1), per_feature(ball_bias), ALU.mult))
                did(e, "mb_sum", row_sum(v(13), by_tile(scr)))
                wait(dve, "a", e, "norms")
                did(e, "floor", nc.vector.tensor_scalar(sm[:, 11:13, :], sm[:, 11:13, :], MIN_NORM, None, ALU.max))
                did(e, "h_clip", nc.vector.tensor_scalar(v(14), v(11), CLIP, None, ALU.min))
                yield 10
                artanh_h = v(24)
                artanh(e, "h_", v(14), artanh_h)
                did(e, "hn_inv", nc.vector.reciprocal(v(25), v(11)))
                did(e, "arg", nc.vector.tensor_tensor(v(25), v(25), v(12), ALU.mult))
                did(e, "arg2", nc.vector.tensor_tensor(v(26), v(25), artanh_h, ALU.mult))
                yield 11
                wait(dve, "a", e, "tanh")
                did(e, "cap", nc.vector.tensor_scalar(v(27), v(27), MAX_NORM, None, ALU.min))
                did(e, "mx_inv", nc.vector.reciprocal(v(28), v(12)))
                did(e, "q", nc.vector.tensor_tensor(v(28), v(27), v(28), ALU.mult))
                did(e, "q_sq", nc.vector.tensor_tensor(v(29), v(28), v(28), ALU.mult))
                did(e, "x2", nc.vector.tensor_tensor(v(29), v(29), v(10), ALU.mult))
                did(e, "xy", nc.vector.tensor_tensor(v(30), v(28), v(13), ALU.mult))
                did(e, "xy1", nc.vector.tensor_scalar(v(30), v(30), 2.0, 1.0, ALU.mult, ALU.add))
                did(e, "top", nc.vector.tensor_scalar(v(31), v(30), bb[:, 6:7], None, ALU.add))
                did(e, "left", nc.vector.tensor_scalar(v(32), v(29), -1.0, 1.0, ALU.mult, ALU.add))
                did(e, "x2y2", nc.vector.tensor_scalar(v(33), v(29), bb[:, 6:7], None, ALU.mult))
                did(e, "den", nc.vector.tensor_tensor(v(33), v(33), v(30), ALU.add))
                did(e, "den_floor", nc.vector.tensor_scalar(v(33), v(33), MIN_NORM, None, ALU.max))
                did(e, "den_inv", nc.vector.reciprocal(v(34), v(33)))
                did(e, "top_q", nc.vector.tensor_tensor(v(31), v(31), v(28), ALU.mult))
                did(e, "a", nc.vector.tensor_tensor(v(31), v(31), v(34), ALU.mult))
                did(e, "c", nc.vector.tensor_tensor(v(32), v(32), v(34), ALU.mult))
                yield 12
                did(e, "a_mx", nc.vector.tensor_tensor(by_tile(scr), nat(1), per_node(v(31)), ALU.mult))
                yield 13
                did(e, "c_bias", nc.vector.tensor_tensor(by_tile(yT), per_feature(ball_bias), per_node(v(32)), ALU.mult))
                did(e, "moved", nc.vector.tensor_tensor(scr, scr, yT, ALU.add))
                yield 14
                wait(dve, "a", e, "m_sq")
                did(e, "m_sum", row_sum(v(9), by_tile(yT)))
                wait(dve, "a", e, "m_norm")
                yield 15
                did(e, "m_floor", nc.vector.tensor_scalar(v(11), v(11), MIN_NORM, None, ALU.max))
                did(e, "m_clip", nc.vector.tensor_scalar(v(14), v(11), MAX_NORM, None, ALU.min))
                artanh(e, "m_", v(14), v(24))
                did(e, "m_inv2", nc.vector.reciprocal(v(25), v(11)))
                did(e, "m_scale", nc.vector.tensor_tensor(v(25), v(25), v(24), ALU.mult))
                did(e, "out", nc.vector.tensor_tensor(half_of(operand[0], half), by_tile(scr), per_node(v(25)), ALU.mult))

            def add_rows(half, src, scale, behind):
                for k in range(HK):
                    ins = nc.vector.scalar_tensor_tensor(res[:, half * HK + k, :], src[:, k, :], scale[:, k:k + 1],
                                                         res[:, half * HK + k, :], ALU.mult, ALU.add)
                    if k == HK // 2 - 1:
                        yield behind
                return ins

            def inverse_sums(e, parts, total):
                did(e, "sum", nc.vector.tensor_tensor(total[:], parts[:, 0, :], parts[:, 1, :], ALU.add))
                did(e, "pos", nc.vector.tensor_scalar(pos[:], total[:], 0.0, None, ALU.is_gt))
                did(e, "masked", nc.vector.tensor_tensor(inv_sum[:], total[:], pos[:], ALU.mult))
                did(e, "one", nc.vector.tensor_scalar(one[:], pos[:], -1.0, 1.0, ALU.mult, ALU.add))
                did(e, "safe", nc.vector.tensor_tensor(inv_sum[:], inv_sum[:], one[:], ALU.add))
                did(e, "inv", nc.vector.reciprocal(inv_sum[:], inv_sum[:]))

            def epilogue(e):
                kind, half = KINDS[e], e % 2
                if kind == "enter":
                    yield from enter(e, half)
                    return
                yield 9 if kind == "last" else 4
                begin(e)
                if kind == "ball":
                    yield 5
                    wait(dve, "a", e, "s_sq")
                    did(e, "s_sum", row_sum(v(9), by_tile(scr)))
                    yield 6
                    wait(dve, "a", e, "s_norm")
                    did(e, "s_floor", nc.vector.tensor_scalar(v(11), v(10), MIN_NORM, None, ALU.max))
                    did(e, "s_inv", nc.vector.reciprocal(v(12), v(11)))
                    did(e, "s_scale", nc.vector.scalar_tensor_tensor(v(12), v(11), ARTANH_MAX_NORM, v(12), ALU.min, ALU.mult))
                    for k in range(HK):
                        ins = nc.vector.tensor_scalar(by_tile(scr)[:, k, :], nat(half)[:, k, :], 0.0, sm[:, 12, k:k + 1],
                                                      ALU.max, ALU.mult)
                        if k == HK // 2 - 1:
                            yield 7
                    did(e, "u", ins)
                    yield 8
                    wait(dve, "a", e, "u_sq")
                    did(e, "u_sum", row_sum(v(13), by_tile(yT)))
                    yield 9
                    wait(dve, "a", e, "u_norm")
                    did(e, "u_floor", nc.vector.tensor_scalar(v(15), v(14), MIN_NORM, None, ALU.max))
                    did(e, "u_inv", nc.vector.reciprocal(v(17), v(15)))
                    wait(dve, "a", e, "u_tanh")
                    did(e, "u_scale", nc.vector.scalar_tensor_tensor(v(18), v(16), MAX_NORM, v(17), ALU.min, ALU.mult))
                    did(e, "res", (yield from add_rows(half, by_tile(scr), v(18), 10)))
                elif kind in ("swish", "swish_norm"):
                    wait(dve, "p", e, "nat")
                    did(e, "biased", nc.vector.tensor_tensor(by_tile(scr), nat(half), per_feature(bias["swish"]), ALU.add))
                    if kind == "swish_norm":
                        yield 7
                        wait(dve, "a", e, "swish")
                        did(e, "res", nc.vector.tensor_tensor(half_of(res, half), half_of(res, half), by_tile(yT), ALU.add))
                elif kind == "columns":
                    wait(dve, "p", e, "nat")
                    dve.wait_ge(hi_ready, NK * 2)
                    inverse_sums(e, col_part, deg)
                    yield 6
                    did(e, "res", (yield from add_rows(half, nat(half), half_of(inv_sum, half), 8)))
                elif kind == "rows":
                    wait(dve, "p", e, "nat")
                    dve.wait_ge(hi_ready, NK * 8)
                    inverse_sums(e, row_part, deg)
                    yield 6
                    wait(dve, "a", e, "droot")
                    did(e, "dinv", nc.vector.reciprocal(dinv[:], droot[:]))
                    yield 7
                    did(e, "res", (yield from add_rows(half, nat(half), half_of(inv_sum, half), 8)))
                elif kind == "embed":
                    wait(dve, "p", e, "nat")
                    for k in range(HK):
                        n_ = half * HK + k
                        ins = nc.vector.scalar_tensor_tensor(by_tile(scr)[:, k, :], nat(half)[:, k, :], dinv[:, n_:n_ + 1],
                                                             bias["embed"][:], ALU.mult, ALU.add)
                        if k == HK // 2 - 1:
                            yield 5
                    did(e, "z", ins)
                    yield 6
                    did(e, "leaky", nc.vector.scalar_tensor_tensor(half_of(z, half), by_tile(scr), 0.1, by_tile(scr),
                                                                   ALU.mult, ALU.max))
                    yield 7
                    wait(dve, "a", e, "z_sq")
                    did(e, "z_sum", row_sum(half_of(z_sq, half), by_tile(yT)))
                elif kind == "last":
                    did(e, "biased", nc.vector.tensor_tensor(half_of(res, half), half_of(res, half),
                                                             per_feature(bias["last"]), ALU.add))
                    yield 12
                    wait(dve, "p", e, "nat")
                    did(e, "out", (yield from add_rows(half, nat(half), half_of(dlast, half), 13)))
                if kind in ("ball", "swish_norm", "rows"):
                    first = {"ball": 11, "swish_norm": 8, "rows": 9}[kind]
                    yield first
                    yield from norm_stats(e, half, first + 1)

            dve.wait_ge(setup_a, 2)
            nc.vector.tensor_scalar(bb[:, 2:3], bb[:, 1:2], MIN_NORM, None, ALU.max).then_inc(setup_v, 1)
            dve.wait_ge(setup_v, 1)
            nc.vector.reciprocal(bb[:, 4:5], bb[:, 2:3]).then_inc(setup_v, 1)
            dve.wait_ge(setup_v, 2)
            dve.wait_ge(setup_a, 3)
            nc.vector.scalar_tensor_tensor(bb[:, 5:6], bb[:, 3:4], MAX_NORM, bb[:, 4:5], ALU.min, ALU.mult).then_inc(setup_v, 1)
            dve.wait_ge(setup_v, 3)
            nc.vector.tensor_scalar(ball_bias[:], bias["ball"][:], bb[:, 5:6], None, ALU.mult).then_inc(setup_v, 1)
            dve.wait_ge(setup_v, 4)
            dve.wait_ge(setup_a, 4)

            for _ in epilogue(0):
                pass

            def sum_near(r, k, i=0):
                kk = k + GROUP * i
                dst = near_sum[:, bass.ds(kk - HK * (k >= HK), 1), :]
                for t in range(TOPK):
                    w = near_w[:, bass.ds(kk, 1), t]
                    if t == 0:
                        dve.wait_ge(fetched[r], 16 * TOPK * (k // GROUP + 1) + 16 * TOPK * i)
                        ins = nc.vector.tensor_scalar(dst, near_rows[:, r, t:t + 1, :], w, None, ALU.mult)
                    else:
                        dve.wait_ge(near_done, TOPK * k + t + TOPK * GROUP * i)
                        ins = nc.vector.scalar_tensor_tensor(dst, near_rows[:, r, t:t + 1, :], w, dst, ALU.mult, ALU.add)
                    ins.then_inc(near_done, 1)

            for s, (mat, half, src, kind) in enumerate(SWEEPS):
                kept = KEPT if mat == "T" else 0

                if s == LAST:
                    for _ in epilogue(s + 1):
                        pass
                    nc.vector.tensor_scalar(neg_sq[:], z_sq[:], -1.0, None, ALU.mult)
                    for h in range(2):
                        dve.wait_ge(za, ZA.index(f"sq{h}") + 1)
                        cols = slice(h * HALF, (h + 1) * HALF)
                        nc.vector.tensor_tensor(zT[:, 1, cols], acc(h), zT[:, 0, cols].bitcast(F32), ALU.subtract
                                                ).then_inc(zv, 1)
                    for h in range(2):
                        dve.wait_ge(za, ZA.index(f"row{h}") + 1)
                        row = sq_row[32:64, h * HALF:(h + 1) * HALF]
                        nc.vector.tensor_tensor(row, acc(h)[32:64, :], row.bitcast(F32), ALU.subtract).then_inc(zv, 1)

                    def settle_a(g, i):
                        b, base = g % 2, len(GV) * g + 2 * len(GV) * i
                        dve.wait_ge(ranked, 2 * GROUP * (g + 1) + 4 * GROUP * i)
                        nc.vector.tensor_scalar(gd[:, b, :, :], top[:, b, :, 0:TOPK], 0.0, -1.0, ALU.min, ALU.mult).then_inc(gv, 1)
                        dve.wait_ge(gv, base + 1)
                        nc.vector.tensor_scalar(gd[:, b, :, :], gd[:, b, :, :], DIST_EPS, None, ALU.add).then_inc(gv, 1)

                    def settle_b(g, i):
                        b, base = g % 2, len(GV) * g + 2 * len(GV) * i
                        k = bass.ds(GROUP * g + 2 * GROUP * i, GROUP)
                        dve.wait_ge(ga, len(GA) * g + GA.index("weight") + 1 + 2 * len(GA) * i)
                        row_sum(gs[:, b, 0, :], near_w[:, k, :]).then_inc(gv, 1)
                        dve.wait_ge(gv, base + 3)
                        nc.vector.tensor_tensor(gs[:, b, 0, :], gs[:, b, 0, :], deg[:, k], ALU.add).then_inc(gv, 1)

                    def settle_c(g, i):
                        b, base = g % 2, len(GV) * g + 2 * len(GV) * i
                        k0 = GROUP * g + 2 * GROUP * i
                        k = bass.ds(k0, GROUP)
                        dve.wait_ge(ga, len(GA) * g + GA.index("root") + 1 + 2 * len(GA) * i)
                        nc.vector.reciprocal(dlast[:, k], gs[:, b, 1, :]).then_inc(gv, 1)
                        dve.wait_ge(gv, base + 5)
                        nc.vector.tensor_tensor(gs[:, b, 2, :], dlast[:, k], droot[:, k], ALU.mult).then_inc(gv, 1)
                        dve.wait_ge(gv, base + 6)
                        for r in range(GROUP):
                            tile = operand[0][:, bass.ds(k0 + r, 1), :]
                            ins = nc.vector.tensor_scalar(tile, tile, gs[:, b, 2, r:r + 1], None, ALU.mult)
                        ins.then_inc(gv, 1)
                        nc.vector.tensor_copy(near_at[:, k, :], top_at[:, b, :, 0:TOPK]).then_inc(gv, 1)

                    def rank(g, i=0):
                        for r in range(GROUP):
                            k = GROUP * g + r
                            dve.wait_ge(zz_out, 4 * (k + 1) + 8 * GROUP * i)
                            if g >= 2 and r == 0:
                                dve.wait_ge(gv, len(GV) * (g - 1) + 2 * len(GV) * i)
                            apart(dve)
                            nc.vector.max(top[:, g % 2, r, :], dist[k % 2][:, :]).then_inc(ranked, 1)
                            dve.wait_ge(ranked, 2 * k + 1 + 4 * GROUP * i)
                            apart(dve)
                            nc.vector.max_index(top_at[:, g % 2, r, :], top[:, g % 2, r, :], dist[k % 2][:, :]
                                                ).then_inc(ranked, 1)
                            if g > 0 and r == 1:
                                settle_b(g - 1, i)
                            if g > 0 and r == 3:
                                settle_c(g - 1, i)
                        settle_a(g, i)

                    rank(0)
                    rank(1)
                    with dve.Fori(0, NG // 2 - 1) as i:
                        rank(2, i)
                        rank(3, i)
                    settle_b(NG - 1, 0)
                    settle_c(NG - 1, 0)

                def split_group(g, i=0):
                    dve.wait_ge(sx_hi, NG * s + g + 1 + (BODY // GROUP) * i)
                    nc.vector.tensor_tensor(split_x[:, g % 2, :, 1, :], operand[src][:, bass.ds(GROUP * g + BODY * i, GROUP), :],
                                            split_x[:, g % 2, :, 0, :].bitcast(F32), ALU.subtract).then_inc(sx_lo, 1)

                def lo_part(t, i=0):
                    tile = kept_tiles[:, half, t, :] if t < kept else raw[:, (first_ring[s] + t) % RAW, :]
                    dve.wait_ge(hi_ready, NK * s + t + 1 + BODY * i)
                    if NK * s + t >= LO:
                        dve.wait_ge(tile_done, NK * s + t - LO + 1 + BODY * i)
                    nc.vector.tensor_tensor(lo[:, t % LO, :], tile, hi[:, t % HI, :].bitcast(F32), ALU.subtract
                                            ).then_inc(lo_ready, 1)

                epi = Woven(None if s == LAST else epilogue(s + 1))
                for t in range(PEELED):
                    if t % GROUP == 0:
                        split_group(t // GROUP)
                    lo_part(t)
                    if s == LAST and t >= BODY and t % 2 == 1:
                        sum_near((t - BODY) // 2, (t - BODY) // 2)
                    if s == LAST + 1 and t % 2 == 1:
                        if t == BODY + 1:
                            wait(dve, "p", s + 1, "near")
                        sum_near(t // 2 % GROUP, HK - GROUP + t // 2)
                    epi.after(t)
                epi.finish()
                with dve.Fori(0, LOOPS) as i:
                    for t in range(PEELED, PEELED + BODY):
                        if t % GROUP == 0:
                            split_group(t // GROUP, i)
                        lo_part(t, i)
                        if s >= LAST and t % 2 == 1:
                            r = (t - PEELED) // 2
                            sum_near(r, r + GROUP + HK * (s - LAST), i)
            for r in range(GROUP):
                sum_near(r, NK - GROUP + r)
            for _ in epilogue(NS + 1):
                pass

        @block.gpsimd
        def _(pool):
            nc.gpsimd.memset(pick_half[:], -0.5).then_inc(setup_g, 1)
            nc.gpsimd.memset(two_rows[:].bitcast(F32), 0.0).then_inc(setup_g, 1)
            pool.wait_ge(setup_g, 2)
            nc.gpsimd.memset(two_rows[0:1, :].bitcast(F32), 1.0).then_inc(setup_g, 1)
            nc.gpsimd.memset(two_rows[32:33, :].bitcast(F32), 1.0).then_inc(setup_g, 1)

            def stage(g, i=0):
                if g >= 2:
                    pool.wait_ge(zz_done, 4 * GROUP * (g - 1) + 8 * GROUP * i)
                cols = bass.ds(GROUP * P * g + 2 * GROUP * P * i, GROUP * P)
                for part in range(2):
                    ins = nc.gpsimd.tensor_copy(split_x[:, g % 2, :, part, :], by_tile(zT[:, part, cols].bitcast(F32)))
                ins.then_inc(z_staged, 1)

            pool.wait_ge(zv, 2)
            pool.wait_ge(tile_done, NK * LAST)
            stage(0)
            stage(1)
            with pool.Fori(0, NG // 2 - 1) as i:
                stage(2, i)
                stage(3, i)

            for q in rows_out:
                pool.wait_ge(q, 16 * NG // 2)
            pool.wait_ge(gv, len(GV) * NG)
            for k in range(NK):
                if k >= GROUP:
                    pool.wait_ge(near_done, TOPK * (k - GROUP + 1))
                for t in range(TOPK):
                    nc.gpsimd.indirect_dma_start(near_rows[:, k % GROUP, t, :], None, rows_dram,
                                                 bass.IndirectOffsetOnAxis(ap=near_at[:, k, t:t + 1], axis=0)
                                                 ).then_inc(fetched[k % GROUP], 16)

        @block.tensor
        def _(pe):
            steps = Steps(pe, "p")

            def epilogue(e):
                kind, half = KINDS[e], e % 2
                bank_half = 1 if kind == "enter" else half
                if kind == "enter":
                    yield 3
                    wait(pe, "a", e, "h")
                    if e == 1:
                        wait(pe, "v", 0, "moved")
                    for k in range(HK):
                        ins = nc.tensor.transpose(nat(1)[:, k, :], by_tile(scr)[:, k, :], weights["ident"][:])
                    steps.did(e, "hT", ins)
                    yield 5
                    wait(pe, "a", e, "hT")
                else:
                    yield 8 if kind == "last" else 1
                    if kind == "last":
                        pe.wait_ge(near_done, TOPK * HK * (half + 1))
                        for k in range(HK):
                            ins = nc.tensor.matmul(nat(half)[:, k, :], near_sum[:, k, :], weights["ident"][:],
                                                   start=False, stop=True, skip_group_check=True)
                        steps.did(e, "near", ins)
                        yield 10
                    wait(pe, "a", e, "yT")
                for k in range(HK):
                    ins = nc.tensor.matmul(nat(bank_half)[:, k, :], by_tile(yT)[:, k, :], weights[WEIGHT[kind]][:],
                                           start=True, stop=True, skip_group_check=True)
                steps.did(e, "nat", ins)

            pe.wait_ge(const_in, 16 * CONSTS)
            for _ in epilogue(0):
                pass

            for s, (mat, half, src, kind) in enumerate(SWEEPS):
                if s == LAST:
                    for _ in epilogue(s + 1):
                        pass
                    pe.wait_ge(setup_g, 4)
                    for h in range(2):
                        wait(pe, "v", s + h, "leaky")
                        wait(pe, "v", s + h, "z")
                        for k in range(HK):
                            ins = nc.tensor.transpose(nat(h)[:, k, :], z[:, h * HK + k, :], weights["ident"][:])
                        ins.then_inc(zp, 1)
                    for h in range(2):
                        pe.wait_ge(za, ZA.index(f"sq{h}") + 1)
                        pe.wait_ge(zv, h + 1)
                        for b in range(4):
                            ins = nc.tensor.matmul(ps[:, 4 * h + b, :], pick_half[:], work[:, h, b * BANK:(b + 1) * BANK],
                                                   start=True, stop=True)
                        ins.then_inc(zp, 1)
                    pe.wait_ge(zv, len(ZV))
                    pe.wait_ge(za, len(ZA))

                    def distances(g, i=0):
                        pe.wait_ge(z_staged, g + 1 + 2 * i)
                        for r in range(GROUP):
                            k = GROUP * g + r
                            for c in range(4):
                                if k >= 1:
                                    pe.wait_ge(zz_out, 4 * (k - 1) + c + 1 + 8 * GROUP * i)
                                for b in (2 * c, 2 * c + 1):
                                    cols = slice(b * BANK, (b + 1) * BANK)
                                    z_hi, z_lo = split_x[:, g % 2, r, 0, :], split_x[:, g % 2, r, 1, :]
                                    nc.tensor.matmul(ps[:, b, :], two_rows[:], sq_row[:, cols], start=True, stop=False)
                                    nc.tensor.matmul(ps[:, b, :], z_lo, zT[:, 0, cols], start=False, stop=False)
                                    nc.tensor.matmul(ps[:, b, :], z_hi, zT[:, 1, cols], start=False, stop=False)
                                    ins = nc.tensor.matmul(ps[:, b, :], z_hi, zT[:, 0, cols], start=False, stop=True)
                                ins.then_inc(zz_done, 1)

                    distances(0)
                    distances(1)
                    with pe.Fori(0, NG // 2 - 1) as i:
                        distances(2, i)
                        distances(3, i)

                if s < 2:
                    wait(pe, "v", s, "moved")
                elif s >= LAST:
                    pe.wait_ge(zz_out, 4 * NK)
                else:
                    who, name = PSUM_READ[KINDS[s]]
                    wait(pe, who, s, name)

                def products(t, i=0):
                    g = t // GROUP
                    if t % GROUP == 0:
                        pe.wait_ge(sx_lo, NG * s + g + 1 + (BODY // GROUP) * i)
                    pe.wait_ge(hi_ready, NK * s + t + 1 + BODY * i)
                    pe.wait_ge(lo_ready, NK * s + t + 1 + BODY * i)
                    x_hi, x_lo = split_x[:, g % 2, t % GROUP, 0, :], split_x[:, g % 2, t % GROUP, 1, :]
                    tile_hi, tile_lo = hi[:, t % HI, :], lo[:, t % LO, :]
                    for j, (w, tile) in enumerate(((x_hi, tile_lo), (x_hi, tile_hi), (x_lo, tile_hi))):
                        for b in range(4):
                            ins = nc.tensor.matmul(ps[:, 4 * half + b, :], w, tile[:, b * BANK:(b + 1) * BANK],
                                                   start=(t == 0 and j == 0), stop=True, skip_group_check=True)
                    ins.then_inc(tile_done, 1)

                epi = Woven(None if s == LAST else epilogue(s + 1))
                for t in range(PEELED):
                    products(t)
                    epi.after(t)
                epi.finish()
                with pe.Fori(0, LOOPS) as i:
                    for t in range(PEELED, PEELED + BODY):
                        products(t, i)
            for _ in epilogue(NS + 1):
                pass


def kernel(x, adj, L0_gnn_weight, L0_gnn_bias, L1_gnn_W, L1_gnn_b, L2_gnn_W_in, L2_gnn_W_out,
           L3_gnn_W1, L3_gnn_b1, L3_gnn_W2, L3_gnn_b2):
    import concourse.bacc as bacc
    from concourse.bass_utils import run_bass_kernel_spmd

    arrays = {
        "x": x, "adj": adj, "adj_t": np.asarray(adj).T, "w_ball_t": np.asarray(L0_gnn_weight).T,
        "b_ball": L0_gnn_bias, "w_swish": L1_gnn_W, "b_swish": L1_gnn_b, "w_in": L2_gnn_W_in,
        "w_out": L2_gnn_W_out, "w_embed": L3_gnn_W1, "b_embed": L3_gnn_b1, "w_last": L3_gnn_W2,
        "b_last": L3_gnn_b2, "eye": np.eye(P, dtype=np.float32)}
    arrays = {n: np.ascontiguousarray(a) for n, a in arrays.items()}
    nc = bacc.Bacc("TRN2", target_bir_lowering=False, num_devices=1)
    args = [nc.dram_tensor(n, a.shape, F32, kind="ExternalInput").ap() for n, a in arrays.items()]
    rows_dram = nc.dram_tensor("rows", (N, P), F32, kind="Internal").ap()
    out = nc.dram_tensor("out", (N, P), F32, kind="ExternalOutput").ap()
    graph_layers(nc, *args, rows_dram, out)
    r = run_bass_kernel_spmd(nc, [arrays], core_ids=[0])
    return r.results[0]["out"]
```

```python
from contextlib import ExitStack

import numpy as np

import concourse.bass as bass
from concourse import mybir
from concourse.alu_op_type import AluOpType as ALU

F32 = mybir.dt.float32
F32R = mybir.dt.float32r
U32 = mybir.dt.uint32
ACT = mybir.ActivationFunctionType
AX_X = mybir.AxisListType.X

P = 128
N = 4096
NK = N // P
HALF = N // 2
HK = NK // 2
BANK = 512
GROUP = 4
NG = NK // GROUP
BODY = 8
PEELED = 16
LOOPS = (NK - PEELED) // BODY
EARLY = 12
RAW, HI, LO = 4, 4, 2
KEPT = (4, 9)
QUARTER = HK // 4
TOPK = 4

MIN_NORM = 1e-15
MAX_NORM = float(np.float32(1.0) - np.float32(0.004))
CLIP = float(np.float32(1.0 - 1e-7))
ARTANH_MAX_NORM = float(np.arctanh(MAX_NORM))
LN_EPS = 1e-5
DIST_EPS = 1e-10

SWEEPS = [("T", 0, 0, "ball"), ("T", 1, 0, "ball"),
          ("T", 0, 1, "swish"), ("T", 1, 1, "swish"),
          ("T", 0, 0, "swish_norm"), ("T", 1, 0, "swish_norm"),
          ("A", 0, 1, "columns"), ("A", 1, 1, "columns"),
          ("T", 0, 1, "rows"), ("T", 1, 1, "rows"),
          ("T", 0, 0, "embed"), ("T", 1, 0, "embed"),
          ("T", 0, 0, "last"), ("T", 1, 0, "last")]
NS = len(SWEEPS)
LAST = NS - 2
SUMMED = (0, 1, 6, 7)
WHOLE = [KEPT] + 11 * [KEPT] + [range(EARLY), (1, 3, 4, 7, 9, 11)]
for _s in range(NS):
    assert max(WHOLE[_s]) < PEELED - RAW

KINDS = ["enter", "none"] + [s[3] for s in SWEEPS]
WEIGHT = {"ball": "ident", "swish": "swish", "swish_norm": "swish", "columns": "out",
          "rows": "in", "embed": "embed", "last": "last"}

NORM_V = ["stats", "diff", "msum", "vsum", "dsq", "var", "vareps", "rstd", "shift"]
ARTANH_V = ["plus", "minus", "inv", "ratio", "sq", "p1", "p2", "p3", "p4", "small", "gap", "pick", "artanh"]

STEPS = {
    "enter": {
        "v": NORM_V + ["hT0", "hT1", "hh", "hh_sum", "mb0", "mb_sum0", "mb1", "mb_sum1", "floor", "h_clip"]
        + ["h_" + n for n in ARTANH_V]
        + ["hn_inv", "arg", "arg2", "cap", "mx_inv", "q", "q_sq", "x2", "xy", "xy1", "top", "left", "x2y2",
           "den", "den_floor", "den_inv", "top_q", "a", "c", "moved0", "moved1", "m_floor", "m_clip"]
        + ["m_" + n for n in ARTANH_V] + ["m_inv2", "m_scale", "out0", "out1"],
        "a": ["std", "h0", "h1", "h_sq0", "mx_sq0", "mx_sq1", "norms", "h_ln", "tanh", "cb0", "cb1",
              "m_sq0", "m_sq1", "m_norm", "m_ln"],
        "p": ["hT0", "hT1", "mx0", "mx1"]},
    "none": {"v": [], "a": [], "p": []},
    "ball": {
        "v": ["s_sum", "s_floor", "s_inv", "s_scale", "u_norm", "u_floor", "u_inv", "u_scale", "scale", "res"]
        + NORM_V,
        "a": ["yT", "s_sq", "relu", "relu_sq", "norms", "u_tanh", "std", "out"], "p": ["nat"]},
    "swish": {"v": ["biased"], "a": ["yT", "out"], "p": ["nat"]},
    "swish_norm": {"v": ["biased", "res"] + NORM_V, "a": ["yT", "swish", "std", "out"], "p": ["nat"]},
    "columns": {"v": ["sum", "pos", "masked", "one", "safe", "inv", "res"], "a": ["yT"], "p": ["nat"]},
    "rows": {"v": ["sum", "pos", "masked", "one", "safe", "inv", "dinv", "res"] + NORM_V
             + ["rstd_d", "shift_d"],
             "a": ["yT", "droot", "std", "out"], "p": ["nat"]},
    "embed": {"v": ["z", "leaky"], "a": ["yT", "z_sq"], "p": ["nat"]},
    "last": {"v": ["biased", "out"], "a": ["yT"], "p": ["near", "nat"]},
}
PSUM_READ = {"ball": ("a", "relu_sq"), "swish": ("v", "biased"),
             "swish_norm": ("v", "biased"), "columns": ("v", "res"), "rows": ("v", "res"),
             "embed": ("v", "z"), "last": ("v", "out")}
OPERAND = {"ball": ("a", "out"), "swish": ("a", "out"),
           "swish_norm": ("a", "out"), "rows": ("a", "out")}
OPERAND_OF = {2: 0, 4: 2, 6: 4, 8: 4, 10: 8}

WHEN = {
    "none": {"a": [], "v": [], "p": []},
    "ball": {"a": [1, 3, 4, 5, 6, 7, 8, 10, 14, 15, 15, 15, 15],
             "v": [3, 8, 10, 10, 11, 12, 13, 13, 13, 14, 14, 15], "p": [0]},
    "swish": {"a": [1, 3], "v": [2], "p": [0]},
    "swish_norm": {"a": [1, 3, 9, 11, 12, 13, 14], "v": [2, 4, 5, 6, 7, 8, 10], "p": [0]},
    "columns": {"a": [1], "v": [2, 3, 4, 5, 6], "p": [0]},
    "rows": {"a": [1, 3, 11, 12, 13, 14, 15], "v": [2, 3, 4, 5, 6, 7, 8, 8, 9, 10, 11], "p": [0]},
    "embed": {"a": [1, 7, 8, 9, 10], "v": [2, 3, 4, 5, 6], "p": [0]},
    "last": {"a": [12], "v": [9, 14, 15, 15, 15], "p": [10, 12]},
}

NEAR_AT = {}
for _k, _at in enumerate([(LAST, t) for t in range(PEELED + 1, PEELED + BODY, 2)]
                         + [None] * GROUP
                         + [(LAST + 1, t) for t in (0, 1, 3, 4, 5, 7, 8, 9, 12, 13, 14, 15)]
                         + [(LAST + 1, t) for t in range(PEELED + 1, PEELED + BODY, 2)]):
    if _at is not None:
        NEAR_AT[_at] = _k

GV = ["neg", "eps", "sum", "total", "dlast", "scale", "operand", "places"]
GA = ["dist", "weight", "root"]
ZP = ["zT0", "zT1", "sq0", "sq1"]
ZA = ["hi0", "sq0", "hi1", "sq1", "row0", "row1"]
ZV = ["lo0", "lo1", "row0", "row1", "zero"]


def step_counts():
    at = {}
    for who in "vap":
        n = 0
        for e, kind in enumerate(KINDS):
            at[who, e, "begin"] = n
            for name in STEPS[kind][who]:
                n += 1
                at[who, e, name] = n
            at[who, e, "end"] = n
    return at


def graph_layers(nc, x, adj, adj_t, w_ball_t, b_ball, w_swish, b_swish, w_in, w_out, w_embed, b_embed,
                 w_last, b_last, eye, rows_dram, out):
    at = step_counts()

    ring_no, tile_at = {}, []
    for s, (mat, _, _, _) in enumerate(SWEEPS):
        for t in range(NK):
            if not (mat == "T" and t in KEPT) or s == LAST:
                ring_no[s, t] = len(tile_at)
                tile_at.append(NK * s + t)

    hi_no, lo_no, sx_no, hi_tile, lo_tile, sx_end = {}, {}, {}, [], [], []
    for s in range(NS):
        for t in range(NK):
            if s in SUMMED or t not in WHOLE[s]:
                hi_no[s, t] = len(hi_tile)
                hi_tile.append(NK * s + t)
            if t not in WHOLE[s]:
                lo_no[s, t] = len(lo_tile)
                lo_tile.append(NK * s + t)
            if t % GROUP == 0 and any(u not in WHOLE[s] for u in range(t, t + GROUP)):
                sx_no[s, t // GROUP] = len(sx_end)
                sx_end.append(NK * s + t + GROUP)

    with ExitStack() as ctx:
        def sb(name, shape, dt=F32):
            return ctx.enter_context(nc.sbuf_tensor(name, shape, dt))

        def sem(name):
            return ctx.enter_context(nc.semaphore(name))

        raw = sb("raw", [P, RAW, HALF])
        kept_tiles = sb("kept_tiles", [P, 2, len(KEPT), HALF])
        hi = sb("hi", [P, HI, HALF], F32R)
        lo = sb("lo", [P, LO, HALF], F32R)
        operand = [sb("operand0", [P, NK, P]), sb("operand1", [P, NK, P])]
        res = sb("res", [P, NK, P])
        work = sb("work", [P, 2, HALF])
        yT, scr = work[:, 0, :], work[:, 1, :]
        split_x = sb("split_x", [P, 2, GROUP, 2, P], F32R)
        weights = {n: sb("weight_" + n, [P, P]) for n in ("ident", "ball", "swish", "in", "out", "embed", "last")}
        bias = {n: sb("bias_" + n, [P, P]) for n in ("ball", "swish", "embed", "last")}
        ball_bias = sb("ball_bias", [P, P])
        bb = sb("bb", [P, 8])
        stats = sb("stats", [P, NK, 6])
        SMALL = 40
        sm = sb("sm", [P, SMALL, NK])
        col_part = sb("col_part", [P, 2, NK])
        row_part = sb("row_part", [P, 2, NK])
        deg, pos, one, inv_sum = (sb(n, [P, NK]) for n in ("deg", "pos", "one", "inv_sum"))
        droot, dinv = sb("droot", [P, NK]), sb("dinv", [P, NK])
        z_sq = sb("z_sq", [P, NK])
        neg_sq = sb("neg_sq", [P, NK])
        pick_half = sb("pick_half", [P, P])
        two_rows = sb("two_rows", [P, P], F32R)
        early_x = sb("early_x", [P, RAW, P])
        top = sb("top", [P, 2, GROUP, 8])
        top_at = sb("top_at", [P, 2, GROUP, 8], U32)
        near_at = sb("near_at", [P, NK, TOPK], U32)
        near_w = sb("near_w", [P, NK, TOPK])
        gd = sb("gd", [P, 2, GROUP, TOPK])
        gs = sb("gs", [P, 2, 3, GROUP])
        dlast = sb("dlast", [P, NK])
        z = operand[1]
        zT = hi[:, :, :].rearrange("p (a b) n -> p a (b n)", a=2)
        sq_row = lo[:, :, :].rearrange("p a n -> p (a n)")
        dist = [operand[1][:, :, :].rearrange("p k f -> p (k f)"),
                work[:, :, :].rearrange("p a n -> p (a n)")]
        rows = operand[1]
        near_rows = operand[1][:, 0:HK, :].rearrange("p (r t) f -> p r t f", t=TOPK)
        near_sum = operand[1][:, HK:NK, :]

        ps = ctx.enter_context(nc.psum_tensor("ps", [P, 8, BANK], F32))

        def by_tile(ap):
            return ap.rearrange("p (k f) -> p k f", f=P)

        def flat(ap):
            return ap.rearrange("p k f -> p (k f)")

        def acc(half):
            return flat(ps[:, 4 * half:4 * half + 4, :])

        def nat(half):
            return by_tile(acc(half))

        def half_of(buf, half):
            return buf[:, half * HK:(half + 1) * HK]

        def per_node(v):
            return v.unsqueeze(2).broadcast_to([P, HK, P])

        def per_feature(v):
            return v[:, :].unsqueeze(1).broadcast_to([P, HK, P])

        def sink(i):
            return hi[:, i, :]

        def flat2(buf):
            return buf[:, :, :].rearrange("p a n -> p (a n)")

        raw_in = [sem(f"raw_in{i}") for i in range(RAW)]
        kept_in = [[sem(f"kept_in{h}_{i}") for i in KEPT] for h in range(2)]
        x_in = [sem("x_in0"), sem("x_in1")]
        const_in = sem("const_in")
        CONSTS = 11
        hi_ready = sem("hi_ready")
        lo_ready = sem("lo_ready")
        tile_done = sem("tile_done")
        sx_hi, sx_lo = sem("sx_hi"), sem("sx_lo")
        step = {"v": sem("v_step"), "a": sem("a_step"), "p": sem("p_step")}
        setup_v, setup_a, setup_g = sem("setup_v"), sem("setup_a"), sem("setup_g")
        zp, za, zv = sem("zp"), sem("za"), sem("zv")
        x_staged = sem("x_staged")
        z_staged = sem("z_staged")
        zz_done = sem("zz_done")
        zz_out = sem("zz_out")
        ranked = sem("ranked")
        gv, ga = sem("gv"), sem("ga")
        rows_out = [sem("rows_out0"), sem("rows_out1")]
        fetched = [sem(f"fetched{i}") for i in range(GROUP)]
        near_scaled = sem("near_scaled")
        near_done = sem("near_done")
        done_out = sem("done_out")
        waited = sem("waited")

        block = ctx.enter_context(nc.Block())

        def wait(eng, who, e, name):
            if at[who, e, name] > 0:
                eng.wait_ge(step[who], at[who, e, name])

        class Steps:

            def __init__(self, eng, who):
                self.eng, self.who, self.count = eng, who, 0

            def did(self, e, name, ins):
                assert at[self.who, e, name] == self.count + 1, (KINDS[e], name)
                self.count += 1
                ins.then_inc(step[self.who], 1)

            def own(self):
                self.eng.wait_ge(step[self.who], self.count)

        class Woven:

            def __init__(self, steps):
                self.steps, self.behind = steps, 0
                if steps is not None:
                    self.behind = next(steps, None)

            def after(self, t):
                while self.behind is not None and self.steps is not None and self.behind <= t:
                    self.behind = next(self.steps, None)

            def finish(self):
                self.after(NK)

        def apart(eng):
            eng.sem_inc(waited)

        def wait_operand(eng, s, half):
            if s >= LAST:
                eng.wait_ge(gv, len(GV) * NG)
                return
            if s < 2:
                wait(eng, "v", 0, f"out{half}")
                return
            e = OPERAND_OF[s - s % 2] + half + 2
            who, name = OPERAND[KINDS[e]]
            wait(eng, who, e, name)

        def wait_tile(eng, s, t, i=0):
            if (s, t) not in ring_no:
                eng.wait_ge(kept_in[SWEEPS[s][1]][KEPT.index(t)], 16)
            else:
                r = ring_no[s, t]
                eng.wait_ge(raw_in[r % RAW], 16 * (r // RAW + 1) + 16 * (BODY // RAW) * i)

        def loaded(s, t):
            if (s, t) not in ring_no:
                return kept_tiles[:, SWEEPS[s][1], KEPT.index(t), :]
            return raw[:, ring_no[s, t] % RAW, :]

        def slot_free(eng, s, t, i, no, tiles, depth):
            if no >= depth:
                before = tiles[no - depth] if t < PEELED else NK * s + t - depth
                eng.wait_ge(tile_done, before + 1 + BODY * i)

        @block.sync
        def _(sp):
            sp.dma_start(res[:, 0:HK, :], x.rearrange("(k p) f -> p k f", p=P)[:, 0:HK, :]).then_inc(x_in[0], 16)
            for name, src in (("ident", eye), ("ball", w_ball_t), ("swish", w_swish), ("in", w_in),
                              ("out", w_out), ("embed", w_embed), ("last", w_last)):
                sp.dma_start(weights[name][:], src).then_inc(const_in, 16)
            for name, src in (("ball", b_ball), ("swish", b_swish), ("embed", b_embed), ("last", b_last)):
                sp.dma_start(bias[name][:], src.rearrange("(a f) -> a f", a=1).broadcast_to([P, P])
                             ).then_inc(const_in, 16)
            sp.dma_start(res[:, HK:NK, :], x.rearrange("(k p) f -> p k f", p=P)[:, HK:NK, :]).then_inc(x_in[1], 16)

            rows_view = rows_dram.rearrange("(k p) f -> p k f", p=P)

            def store_rows(g, i=0):
                sp.wait_ge(gv, len(GV) * g + GV.index("operand") + 1 + 2 * len(GV) * i)
                apart(sp)
                if g >= 2:
                    sp.wait_ge(rows_out[g % 2], 16 * (g // 2) + 16 * i)
                apart(sp)
                k = bass.ds(GROUP * g + 2 * GROUP * i, GROUP)
                sp.dma_start(rows_view[:, k, :], operand[0][:, k, :]).then_inc(rows_out[g % 2], 16)

            for s, (mat, half, _, _) in enumerate(SWEEPS):
                src = {"T": adj_t, "A": adj}[mat]

                def load(t, i=0):
                    r = ring_no[s, t]
                    if r >= RAW:
                        before = tile_at[r - RAW] if t < PEELED else NK * s + t - RAW
                        s_, t_ = before // NK, before % NK
                        if t_ in WHOLE[s_]:
                            sp.wait_ge(tile_done, before + 1)
                        else:
                            sp.wait_ge(lo_ready, lo_no[s_, t_] + 1 + BODY * i)
                    sp.dma_start(raw[:, r % RAW, :],
                                 src[bass.ds((t + BODY * i) * P, P), half * HALF:(half + 1) * HALF]
                                 ).then_inc(raw_in[r % RAW], 16)

                if s == LAST:
                    def load_next(j, i):
                        sp.wait_ge(tile_done, NK * s + j + 1 + RAW * i)
                        r = ring_no[s, j]
                        sp.dma_start(raw[:, r % RAW, :],
                                     src[bass.ds((RAW + j + RAW * i) * P, P), half * HALF:(half + 1) * HALF]
                                     ).then_inc(raw_in[r % RAW], 16)

                    for t in range(RAW):
                        load(t)
                    store_rows(0)
                    store_rows(1)
                    with sp.Fori(0, NG // 2 - 1) as i:
                        load_next(0, i)
                        load_next(1, i)
                        store_rows(2, i)
                        load_next(2, i)
                        load_next(3, i)
                        store_rows(3, i)
                else:
                    for t in range(PEELED):
                        if (s, t) in ring_no:
                            load(t)
                        elif s < 2:
                            sp.dma_start(kept_tiles[:, half, KEPT.index(t), :],
                                         src[t * P:(t + 1) * P, half * HALF:(half + 1) * HALF]
                                         ).then_inc(kept_in[half][KEPT.index(t)], 16)
                with sp.Fori(0, LOOPS) as i:
                    for t in range(PEELED, PEELED + BODY):
                        load(t, i)

            for h in range(2):
                wait(sp, "v", NS + h, "out")
                sp.dma_start(out.rearrange("(k p) f -> p k f", p=P)[:, h * HK:(h + 1) * HK, :],
                             half_of(res, h)).then_inc(done_out, 16)
            sp.wait_ge(done_out, 32)

        @block.scalar
        def _(act):
            steps = Steps(act, "a")
            did = steps.did

            def v(i):
                return sm[:, i, 0:HK]

            def w(i):
                return sm[:, i, :]

            def begin(e):
                for who in "vp":
                    wait(act, who, e, "begin")
                if e > 0:
                    steps.own()

            def normalise(e, dst, name, when):
                yield next(when)
                wait(act, "v", e, "vareps")
                did(e, "std", nc.scalar.activation(v(6), v(5), ACT.Sqrt))
                for k in range(HK):
                    if k % QUARTER == 0:
                        yield next(when)
                    if k == 0:
                        wait(act, "v", e, "shift_d" if KINDS[e] == "rows" else "shift")
                    ins = nc.scalar.activation(dst[:, k, :], res[:, e % 2 * HK + k, :], ACT.Relu,
                                               scale=sm[:, 7, k:k + 1], bias=sm[:, 8, k:k + 1])
                did(e, name, ins)

            def square_sums(e, name, dst, src, sums, when=None, ready=None):
                for k in range(HK):
                    if when is not None and k % QUARTER == 0:
                        yield next(when)
                    if ready is not None and k == 0:
                        ready()
                    ins = nc.scalar.activation(dst[:, k, :], src[:, k, :], ACT.Square, accum_out=sums[:, k:k + 1])
                did(e, name, ins)
                steps.own()

            def epilogue(e):
                kind, half = KINDS[e], e % 2
                if kind == "none":
                    return
                when = iter(WHEN[kind]["a"])
                yield next(when)
                begin(e)
                act.wait_ge(tile_done, NK * (e - 1))
                if kind == "last":
                    wait(act, "p", e, "near")
                did(e, "yT", nc.scalar.copy(yT, acc(half)))
                if kind == "ball":
                    yield next(when)
                    wait(act, "p", e, "nat")
                    did(e, "s_sq", nc.scalar.activation(scr, acc(half), ACT.Square))
                    yield next(when)
                    did(e, "relu", nc.scalar.activation(yT, acc(half), ACT.Relu))
                    steps.own()
                    yield from square_sums(e, "relu_sq", nat(half), by_tile(yT), v(10), when)
                    wait(act, "v", e, "s_sum")
                    did(e, "norms", nc.scalar.activation(sm[:, 11:13, :], sm[:, 9:11, :], ACT.Sqrt))
                    yield next(when)
                    wait(act, "v", e, "u_floor")
                    did(e, "u_tanh", nc.scalar.activation(v(16), v(15), ACT.Tanh))
                elif kind in ("swish", "swish_norm"):
                    yield next(when)
                    wait(act, "v", e, "biased")
                    if kind == "swish":
                        did(e, "out", nc.scalar.activation(half_of(operand[0], half), by_tile(scr), ACT.Silu))
                    else:
                        did(e, "swish", nc.scalar.activation(yT, scr, ACT.Silu))
                elif kind == "rows":
                    yield next(when)
                    wait(act, "v", e, "sum")
                    did(e, "droot", nc.scalar.activation(droot[:], deg[:], ACT.Sqrt))
                elif kind == "embed":
                    yield from square_sums(e, "z_sq", by_tile(yT), half_of(z, half), half_of(z_sq, half), when,
                                           lambda: wait(act, "v", e, "leaky"))
                if kind in ("ball", "swish_norm", "rows"):
                    dst = operand[0 if kind == "rows" else 1]
                    yield from normalise(e, half_of(dst, half), "out", when)

            def enter():
                wait(act, "v", 0, "vareps")
                did(0, "std", nc.scalar.activation(w(6), w(5), ACT.Sqrt))
                wait(act, "v", 0, "shift")
                for h in range(2):
                    for k in range(h * HK, (h + 1) * HK):
                        ins = nc.scalar.activation(rows[:, k, :], res[:, k, :], ACT.Relu,
                                                   scale=sm[:, 7, k:k + 1], bias=sm[:, 8, k:k + 1])
                    did(0, f"h{h}", ins)
                steps.own()
                for _ in square_sums(0, "h_sq0", by_tile(sink(0)), half_of(rows, 0), w(9)[:, 0:HK]):
                    pass
                for h in range(2):
                    wait(act, "p", 0, f"mx{h}")
                    for _ in square_sums(0, f"mx_sq{h}", by_tile(sink(1 + h)), nat(h), half_of(w(10), h)):
                        pass
                wait(act, "v", 0, "hh_sum")
                did(0, "norms", nc.scalar.activation(sm[:, 11:13, :], sm[:, 9:11, :], ACT.Sqrt))
                wait(act, "v", 0, "h_ratio")
                did(0, "h_ln", nc.scalar.activation(w(19), w(18), ACT.Ln))
                wait(act, "v", 0, "arg2")
                did(0, "tanh", nc.scalar.activation(w(27), w(26), ACT.Tanh))
                wait(act, "v", 0, "c")
                for h in range(2):
                    for k in range(h * HK, (h + 1) * HK):
                        ins = nc.scalar.activation(by_tile(flat2(work))[:, k, :], ball_bias[:], ACT.Copy,
                                                   scale=sm[:, 32, k:k + 1])
                    did(0, f"cb{h}", ins)
                steps.own()
                for h in range(2):
                    wait(act, "v", 0, f"moved{h}")
                    for _ in square_sums(0, f"m_sq{h}", by_tile(sink(3 * (1 - h))), half_of(rows, h),
                                         half_of(w(9), h)):
                        pass
                did(0, "m_norm", nc.scalar.activation(w(11), w(9), ACT.Sqrt))
                wait(act, "v", 0, "m_ratio")
                did(0, "m_ln", nc.scalar.activation(w(19), w(18), ACT.Ln))

            act.wait_ge(const_in, 16 * CONSTS)
            nc.scalar.activation(ball_bias[:], bias["ball"][:], ACT.Square, accum_out=bb[:, 0:1]).then_inc(setup_a, 1)
            act.wait_ge(setup_a, 1)
            nc.scalar.activation(bb[:, 1:2], bb[:, 0:1], ACT.Sqrt).then_inc(setup_a, 1)
            act.wait_ge(setup_v, 1)
            nc.scalar.activation(bb[:, 3:4], bb[:, 2:3], ACT.Tanh).then_inc(setup_a, 1)
            act.wait_ge(setup_v, 4)
            nc.scalar.activation(scr[:, 0:P], ball_bias[:], ACT.Square, accum_out=bb[:, 6:7]).then_inc(setup_a, 1)
            act.wait_ge(setup_a, 4)
            enter()

            def scale_near(k, i=0):
                r = k % GROUP
                act.wait_ge(fetched[r], 16 * TOPK * (k // GROUP + 1) + 16 * TOPK * i)
                apart(act)
                for t in range(TOPK):
                    ins = nc.scalar.activation(near_rows[:, r, t, :], near_rows[:, r, t, :], ACT.Copy,
                                               scale=near_w[:, bass.ds(k + GROUP * i, 1), t])
                ins.then_inc(near_scaled, 1)

            for s, (mat, half, src, kind) in enumerate(SWEEPS):
                sums = {"T": col_part, "A": row_part}[mat]

                if s == LAST:
                    for _ in epilogue(s + 1):
                        pass
                    for h in range(2):
                        sq_buf = work[:, h, :]
                        act.wait_ge(zp, ZP.index(f"zT{h}") + 1)
                        if h == 0:
                            wait(act, "v", s + 1, "end")
                            act.wait_ge(tile_done, NK * s)
                        nc.scalar.copy(zT[:, 0, h * HALF:(h + 1) * HALF], acc(h)).then_inc(za, 1)
                        nc.scalar.activation(sq_buf, acc(h), ACT.Square).then_inc(za, 1)
                    for h in range(2):
                        act.wait_ge(zp, ZP.index(f"sq{h}") + 1)
                        nc.scalar.copy(sq_row[:, h * HALF:(h + 1) * HALF], acc(h)).then_inc(za, 1)

                    def weigh(g, i):
                        act.wait_ge(gv, len(GV) * g + GV.index("eps") + 1 + 2 * len(GV) * i)
                        nc.scalar.activation(gd[:, g % 2, :, :], gd[:, g % 2, :, :], ACT.Sqrt).then_inc(ga, 1)
                        act.wait_ge(ga, len(GA) * g + 1 + 2 * len(GA) * i)
                        k = bass.ds(GROUP * g + 2 * GROUP * i, GROUP)
                        nc.scalar.activation(near_w[:, k, :], gd[:, g % 2, :, :], ACT.Exp, scale=-0.5).then_inc(ga, 1)

                    def root(g, i):
                        act.wait_ge(gv, len(GV) * g + GV.index("total") + 1 + 2 * len(GV) * i)
                        nc.scalar.activation(gs[:, g % 2, 1, :], gs[:, g % 2, 0, :], ACT.Sqrt).then_inc(ga, 1)

                    def leave(g, i=0):
                        for r in range(GROUP):
                            k = GROUP * g + r
                            for c in range(4):
                                act.wait_ge(zz_done, 4 * k + c + 1 + 8 * GROUP * i)
                                if c == 0 and k >= 2:
                                    act.wait_ge(ranked, 2 * (k - 1) + 4 * GROUP * i)
                                apart(act)
                                nc.scalar.activation(dist[k % 2][:, c * 2 * BANK:(c + 1) * 2 * BANK],
                                                     ps[:, 4 + c % 2 * 2:6 + c % 2 * 2, :].rearrange("p b n -> p (b n)"),
                                                     ACT.Identity, bias=neg_sq[:, bass.ds(k + 2 * GROUP * i, 1)],
                                                     scale=2.0).then_inc(zz_out, 1)
                            if g > 0 and r == 0:
                                weigh(g - 1, i)
                            if g > 0 and r == 2:
                                root(g - 1, i)

                    act.wait_ge(zv, len(ZV))
                    act.wait_ge(zp, len(ZP))
                    leave(0)
                    leave(1)
                    with act.Fori(0, NG // 2 - 1) as i:
                        leave(2, i)
                        leave(3, i)
                    weigh(NG - 1, 0)
                    root(NG - 1, 0)

                def split_group(g, i=0):
                    if GROUP * g < PEELED:
                        wait_operand(act, s, g // (NG // 2))
                    n = sx_no[s, g]
                    if n >= 2:
                        before = sx_end[n - 2] if GROUP * g < PEELED else NK * s + GROUP * (g - 1)
                        act.wait_ge(tile_done, before + BODY * i)
                    nc.scalar.copy(split_x[:, n % 2, :, 0, :], operand[src][:, bass.ds(GROUP * g + BODY * i, GROUP), :]
                                   ).then_inc(sx_hi, 1)

                def hi_part(t, i=0):
                    n, tile = hi_no[s, t], loaded(s, t)
                    wait_tile(act, s, t, i)
                    slot_free(act, s, t, i, n, hi_tile, HI)
                    if s in SUMMED:
                        nc.scalar.activation(hi[:, n % HI, :], tile, ACT.Identity,
                                             accum_out=sums[:, half, bass.ds(t + BODY * i, 1)]).then_inc(hi_ready, 1)
                    else:
                        nc.scalar.copy(hi[:, n % HI, :], tile).then_inc(hi_ready, 1)

                if s == LAST:
                    act.wait_ge(zz_done, 4 * NK)
                epi = Woven(None if s == LAST else epilogue(s + 1))
                for t in range(PEELED):
                    if (s, t // GROUP) in sx_no and t % GROUP == 0:
                        split_group(t // GROUP)
                    if (s, t) in hi_no:
                        hi_part(t)
                    if (s, t) in NEAR_AT:
                        scale_near(NEAR_AT[s, t])
                    epi.after(t)
                epi.finish()
                wait_operand(act, s, 1)
                with act.Fori(0, LOOPS) as i:
                    for t in range(PEELED, PEELED + BODY):
                        if t % GROUP == 0:
                            split_group(t // GROUP, i)
                        hi_part(t, i)
                        if (s, t) in NEAR_AT:
                            scale_near(NEAR_AT[s, t], i)
            for k in range(NK - GROUP, NK):
                scale_near(k)
            for _ in epilogue(NS + 1):
                pass

        @block.vector
        def _(dve):
            steps = Steps(dve, "v")

            def v(i):
                return sm[:, i, 0:HK]

            def w(i):
                return sm[:, i, :]

            def did(e, name, ins):
                steps.did(e, name, ins)
                steps.own()

            def row_sum(dst, src):
                return nc.vector.tensor_reduce(dst, src, AX_X, ALU.add)

            def begin(e):
                for who in "ap":
                    wait(dve, who, e, "begin")

            def norm_stats(e, tiles, v, when):
                for i, k in enumerate(tiles):
                    if i % QUARTER == 0:
                        yield next(when, None)
                    ins = nc.vector.bn_stats(stats[:, i, :], res[:, k, :])
                st = stats[:, 0:len(tiles), :]
                did(e, "stats", ins)
                did(e, "diff", nc.vector.tensor_tensor(v(0), st[:, :, 1], st[:, :, 4], ALU.subtract))
                did(e, "msum", nc.vector.tensor_tensor(v(1), st[:, :, 1], st[:, :, 4], ALU.add))
                did(e, "vsum", nc.vector.tensor_tensor(v(2), st[:, :, 2], st[:, :, 5], ALU.add))
                did(e, "dsq", nc.vector.tensor_tensor(v(3), v(0), v(0), ALU.mult))
                did(e, "var", nc.vector.scalar_tensor_tensor(v(4), v(3), P / 4.0, v(2), ALU.mult, ALU.add))
                did(e, "vareps", nc.vector.tensor_scalar(v(5), v(4), 1.0 / P, LN_EPS, ALU.mult, ALU.add))
                yield next(when, None)
                wait(dve, "a", e, "std")
                did(e, "rstd", nc.vector.reciprocal(v(7), v(6)))
                did(e, "shift", nc.vector.scalar_tensor_tensor(v(8), v(1), -0.5, v(7), ALU.mult, ALU.mult))
                if KINDS[e] == "rows":
                    half = e % 2
                    did(e, "rstd_d", nc.vector.tensor_tensor(v(7), v(7), half_of(dinv, half), ALU.mult))
                    did(e, "shift_d", nc.vector.tensor_tensor(v(8), v(8), half_of(dinv, half), ALU.mult))

            def artanh(e, pre, u, dst):
                did(e, pre + "plus", nc.vector.tensor_scalar(w(15), u, 1.0, None, ALU.add))
                did(e, pre + "minus", nc.vector.tensor_scalar(w(16), u, -1.0, 1.0, ALU.mult, ALU.add))
                did(e, pre + "inv", nc.vector.reciprocal(w(17), w(16)))
                did(e, pre + "ratio", nc.vector.tensor_tensor(w(18), w(15), w(17), ALU.mult))
                did(e, pre + "sq", nc.vector.tensor_tensor(w(20), u, u, ALU.mult))
                did(e, pre + "p1", nc.vector.tensor_scalar(w(21), w(20), 1.0 / 7, 1.0 / 5, ALU.mult, ALU.add))
                did(e, pre + "p2", nc.vector.tensor_tensor(w(21), w(21), w(20), ALU.mult))
                did(e, pre + "p3", nc.vector.scalar_tensor_tensor(w(21), w(21), 1.0 / 3, w(20), ALU.add, ALU.mult))
                did(e, pre + "p4", nc.vector.scalar_tensor_tensor(w(21), w(21), 1.0, u, ALU.add, ALU.mult))
                did(e, pre + "small", nc.vector.tensor_scalar(w(22), u, 0.1, None, ALU.is_lt))
                wait(dve, "a", e, pre + "ln")
                did(e, pre + "gap", nc.vector.scalar_tensor_tensor(w(23), w(19), -0.5, w(21), ALU.mult, ALU.add))
                did(e, pre + "pick", nc.vector.tensor_tensor(w(23), w(23), w(22), ALU.mult))
                did(e, pre + "artanh", nc.vector.scalar_tensor_tensor(dst, w(19), 0.5, w(23), ALU.mult, ALU.add))

            def enter():
                for h in range(2):
                    dve.wait_ge(x_in[h], 16)
                for _ in norm_stats(0, range(NK), w, iter(())):
                    pass
                for h in range(2):
                    wait(dve, "p", 0, f"hT{h}")
                    did(0, f"hT{h}", nc.vector.tensor_copy(work[:, h, :], acc(h)))
                pad = [flat(half_of(operand[0], h)) for h in range(2)]
                did(0, "hh", nc.vector.tensor_tensor(by_tile(pad[1]), half_of(rows, 1), half_of(rows, 1), ALU.mult))
                did(0, "hh_sum", row_sum(half_of(w(9), 1), by_tile(pad[1])))
                for h in range(2):
                    wait(dve, "a", 0, f"mx_sq{h}")
                    did(0, f"mb{h}", nc.vector.tensor_tensor(by_tile(pad[h]), nat(h), per_feature(ball_bias), ALU.mult))
                    did(0, f"mb_sum{h}", row_sum(half_of(w(13), h), by_tile(pad[h])))
                wait(dve, "a", 0, "norms")
                did(0, "floor", nc.vector.tensor_scalar(sm[:, 11:13, :], sm[:, 11:13, :], MIN_NORM, None, ALU.max))
                did(0, "h_clip", nc.vector.tensor_scalar(w(14), w(11), CLIP, None, ALU.min))
                artanh_h = w(24)
                artanh(0, "h_", w(14), artanh_h)
                did(0, "hn_inv", nc.vector.reciprocal(w(25), w(11)))
                did(0, "arg", nc.vector.tensor_tensor(w(25), w(25), w(12), ALU.mult))
                did(0, "arg2", nc.vector.tensor_tensor(w(26), w(25), artanh_h, ALU.mult))
                wait(dve, "a", 0, "tanh")
                did(0, "cap", nc.vector.tensor_scalar(w(27), w(27), MAX_NORM, None, ALU.min))
                did(0, "mx_inv", nc.vector.reciprocal(w(28), w(12)))
                did(0, "q", nc.vector.tensor_tensor(w(28), w(27), w(28), ALU.mult))
                did(0, "q_sq", nc.vector.tensor_tensor(w(29), w(28), w(28), ALU.mult))
                did(0, "x2", nc.vector.tensor_tensor(w(29), w(29), w(10), ALU.mult))
                did(0, "xy", nc.vector.tensor_tensor(w(30), w(28), w(13), ALU.mult))
                did(0, "xy1", nc.vector.tensor_scalar(w(30), w(30), 2.0, 1.0, ALU.mult, ALU.add))
                did(0, "top", nc.vector.tensor_scalar(w(31), w(30), bb[:, 6:7], None, ALU.add))
                did(0, "left", nc.vector.tensor_scalar(w(32), w(29), -1.0, 1.0, ALU.mult, ALU.add))
                did(0, "x2y2", nc.vector.tensor_scalar(w(33), w(29), bb[:, 6:7], None, ALU.mult))
                did(0, "den", nc.vector.tensor_tensor(w(33), w(33), w(30), ALU.add))
                did(0, "den_floor", nc.vector.tensor_scalar(w(33), w(33), MIN_NORM, None, ALU.max))
                did(0, "den_inv", nc.vector.reciprocal(w(34), w(33)))
                did(0, "top_q", nc.vector.tensor_tensor(w(31), w(31), w(28), ALU.mult))
                did(0, "a", nc.vector.tensor_tensor(w(31), w(31), w(34), ALU.mult))
                did(0, "c", nc.vector.tensor_tensor(w(32), w(32), w(34), ALU.mult))
                for h in range(2):
                    wait(dve, "a", 0, f"cb{h}")
                    for k in range(HK):
                        n_ = h * HK + k
                        ins = nc.vector.scalar_tensor_tensor(rows[:, n_, :], nat(h)[:, k, :], sm[:, 31, n_:n_ + 1],
                                                             by_tile(flat2(work))[:, n_, :], ALU.mult, ALU.add)
                    did(0, f"moved{h}", ins)
                wait(dve, "a", 0, "m_norm")
                did(0, "m_floor", nc.vector.tensor_scalar(w(11), w(11), MIN_NORM, None, ALU.max))
                did(0, "m_clip", nc.vector.tensor_scalar(w(14), w(11), MAX_NORM, None, ALU.min))
                artanh(0, "m_", w(14), w(24))
                did(0, "m_inv2", nc.vector.reciprocal(w(25), w(11)))
                did(0, "m_scale", nc.vector.tensor_tensor(w(25), w(25), w(24), ALU.mult))
                for h in range(2):
                    did(0, f"out{h}", nc.vector.tensor_tensor(half_of(operand[0], h), half_of(rows, h),
                                                              per_node(half_of(w(25), h)), ALU.mult))

            def add_rows(half, src, scale, when, ready=None):
                for k in range(HK):
                    if k % QUARTER == 0:
                        yield next(when)
                    if ready is not None and k == 0:
                        ready()
                    ins = nc.vector.scalar_tensor_tensor(res[:, half * HK + k, :], src[:, k, :], scale[:, k:k + 1],
                                                         res[:, half * HK + k, :], ALU.mult, ALU.add)
                return ins

            def inverse_sums(e, parts, total):
                did(e, "sum", nc.vector.tensor_tensor(total[:], parts[:, 0, :], parts[:, 1, :], ALU.add))
                did(e, "pos", nc.vector.tensor_scalar(pos[:], total[:], 0.0, None, ALU.is_gt))
                did(e, "masked", nc.vector.tensor_tensor(inv_sum[:], total[:], pos[:], ALU.mult))
                did(e, "one", nc.vector.tensor_scalar(one[:], pos[:], -1.0, 1.0, ALU.mult, ALU.add))
                did(e, "safe", nc.vector.tensor_tensor(inv_sum[:], inv_sum[:], one[:], ALU.add))
                did(e, "inv", nc.vector.reciprocal(inv_sum[:], inv_sum[:]))

            def epilogue(e):
                kind, half = KINDS[e], e % 2
                if kind == "none":
                    return
                when = iter(WHEN[kind]["v"])
                yield next(when)
                begin(e)
                if kind == "ball":
                    wait(dve, "a", e, "s_sq")
                    did(e, "s_sum", row_sum(v(9), by_tile(scr)))
                    yield next(when)
                    wait(dve, "a", e, "norms")
                    did(e, "s_floor", nc.vector.tensor_scalar(v(13), v(11), MIN_NORM, None, ALU.max))
                    did(e, "s_inv", nc.vector.reciprocal(v(14), v(13)))
                    did(e, "s_scale", nc.vector.scalar_tensor_tensor(v(14), v(13), ARTANH_MAX_NORM, v(14), ALU.min, ALU.mult))
                    did(e, "u_norm", nc.vector.tensor_tensor(v(15), v(12), v(14), ALU.mult))
                    did(e, "u_floor", nc.vector.tensor_scalar(v(15), v(15), MIN_NORM, None, ALU.max))
                    did(e, "u_inv", nc.vector.reciprocal(v(17), v(15)))
                    yield next(when)
                    wait(dve, "a", e, "u_tanh")
                    did(e, "u_scale", nc.vector.scalar_tensor_tensor(v(18), v(16), MAX_NORM, v(17), ALU.min, ALU.mult))
                    did(e, "scale", nc.vector.tensor_tensor(v(18), v(18), v(14), ALU.mult))
                    did(e, "res", (yield from add_rows(half, by_tile(yT), v(18), when)))
                elif kind in ("swish", "swish_norm"):
                    wait(dve, "p", e, "nat")
                    did(e, "biased", nc.vector.tensor_tensor(by_tile(scr), nat(half), per_feature(bias["swish"]), ALU.add))
                    if kind == "swish_norm":
                        yield next(when)
                        wait(dve, "a", e, "swish")
                        did(e, "res", nc.vector.tensor_tensor(half_of(res, half), half_of(res, half), by_tile(yT), ALU.add))
                elif kind == "columns":
                    wait(dve, "p", e, "nat")
                    dve.wait_ge(hi_ready, hi_no[1, NK - 1] + 1)
                    inverse_sums(e, col_part, deg)
                    did(e, "res", (yield from add_rows(half, nat(half), half_of(inv_sum, half), when)))
                elif kind == "rows":
                    wait(dve, "p", e, "nat")
                    dve.wait_ge(hi_ready, hi_no[7, NK - 1] + 1)
                    inverse_sums(e, row_part, deg)
                    yield next(when)
                    wait(dve, "a", e, "droot")
                    did(e, "dinv", nc.vector.reciprocal(dinv[:], droot[:]))
                    did(e, "res", (yield from add_rows(half, nat(half), half_of(inv_sum, half), when)))
                elif kind == "embed":
                    wait(dve, "p", e, "nat")
                    for k in range(HK):
                        if k % QUARTER == 0 and k > 0:
                            yield next(when)
                        n_ = half * HK + k
                        ins = nc.vector.scalar_tensor_tensor(by_tile(scr)[:, k, :], nat(half)[:, k, :], dinv[:, n_:n_ + 1],
                                                             bias["embed"][:], ALU.mult, ALU.add)
                    did(e, "z", ins)
                    yield next(when)
                    did(e, "leaky", nc.vector.scalar_tensor_tensor(half_of(z, half), by_tile(scr), 0.1, by_tile(scr),
                                                                   ALU.mult, ALU.max))
                elif kind == "last":
                    did(e, "biased", nc.vector.tensor_tensor(half_of(res, half), half_of(res, half),
                                                             per_feature(bias["last"]), ALU.add))
                    did(e, "out", (yield from add_rows(half, nat(half), half_of(dlast, half), when,
                                                       lambda: wait(dve, "p", e, "nat"))))
                if kind in ("ball", "swish_norm", "rows"):
                    yield from norm_stats(e, range(half * HK, (half + 1) * HK), v, when)

            dve.wait_ge(setup_a, 2)
            nc.vector.tensor_scalar(bb[:, 2:3], bb[:, 1:2], MIN_NORM, None, ALU.max).then_inc(setup_v, 1)
            dve.wait_ge(setup_v, 1)
            nc.vector.reciprocal(bb[:, 4:5], bb[:, 2:3]).then_inc(setup_v, 1)
            dve.wait_ge(setup_v, 2)
            dve.wait_ge(setup_a, 3)
            nc.vector.scalar_tensor_tensor(bb[:, 5:6], bb[:, 3:4], MAX_NORM, bb[:, 4:5], ALU.min, ALU.mult).then_inc(setup_v, 1)
            dve.wait_ge(setup_v, 3)
            nc.vector.tensor_scalar(ball_bias[:], bias["ball"][:], bb[:, 5:6], None, ALU.mult).then_inc(setup_v, 1)
            dve.wait_ge(setup_v, 4)
            dve.wait_ge(setup_a, 4)

            enter()

            def sum_near(k, i=0):
                if k == HK:
                    wait(dve, "p", NS, "near")
                near = near_rows[:, k % GROUP, :, :]
                dve.wait_ge(near_scaled, k + 1 + GROUP * i)
                nc.vector.tensor_tensor(near[:, 0:2, :], near[:, 0:2, :], near[:, 2:4, :], ALU.add).then_inc(near_done, 1)
                dve.wait_ge(near_done, 2 * k + 1 + 2 * GROUP * i)
                nc.vector.tensor_tensor(near_sum[:, bass.ds(k % HK + GROUP * i, 1), :], near[:, 0:1, :], near[:, 1:2, :],
                                        ALU.add).then_inc(near_done, 1)

            for s, (mat, half, src, kind) in enumerate(SWEEPS):
                if s == LAST:
                    for _ in epilogue(s + 1):
                        pass
                    wait(dve, "a", s + 1, "z_sq")
                    nc.vector.tensor_scalar(neg_sq[:], z_sq[:], -1.0, None, ALU.mult)
                    for h in range(2):
                        dve.wait_ge(za, ZA.index(f"sq{h}") + 1)
                        cols = slice(h * HALF, (h + 1) * HALF)
                        nc.vector.tensor_tensor(zT[:, 1, cols], acc(h), zT[:, 0, cols].bitcast(F32), ALU.subtract
                                                ).then_inc(zv, 1)
                    for h in range(2):
                        dve.wait_ge(za, ZA.index(f"row{h}") + 1)
                        row = sq_row[32:64, h * HALF:(h + 1) * HALF]
                        nc.vector.tensor_tensor(row, acc(h)[32:64, :], row.bitcast(F32), ALU.subtract).then_inc(zv, 1)

                    dve.wait_ge(zv, ZV.index("row1") + 1)
                    nc.vector.memset(acc(0), 0.0).then_inc(zv, 1)

                    def settle_a(g, i):
                        b, base = g % 2, len(GV) * g + 2 * len(GV) * i
                        dve.wait_ge(ranked, 2 * GROUP * (g + 1) + 4 * GROUP * i)
                        nc.vector.tensor_scalar(gd[:, b, :, :], top[:, b, :, 0:TOPK], 0.0, -1.0, ALU.min, ALU.mult).then_inc(gv, 1)
                        dve.wait_ge(gv, base + 1)
                        nc.vector.tensor_scalar(gd[:, b, :, :], gd[:, b, :, :], DIST_EPS, None, ALU.add).then_inc(gv, 1)

                    def settle_b(g, i):
                        b, base = g % 2, len(GV) * g + 2 * len(GV) * i
                        k = bass.ds(GROUP * g + 2 * GROUP * i, GROUP)
                        dve.wait_ge(ga, len(GA) * g + GA.index("weight") + 1 + 2 * len(GA) * i)
                        row_sum(gs[:, b, 0, :], near_w[:, k, :]).then_inc(gv, 1)
                        dve.wait_ge(gv, base + 3)
                        nc.vector.tensor_tensor(gs[:, b, 0, :], gs[:, b, 0, :], deg[:, k], ALU.add).then_inc(gv, 1)

                    def settle_c(g, i):
                        b, base = g % 2, len(GV) * g + 2 * len(GV) * i
                        k0 = GROUP * g + 2 * GROUP * i
                        k = bass.ds(k0, GROUP)
                        dve.wait_ge(ga, len(GA) * g + GA.index("root") + 1 + 2 * len(GA) * i)
                        nc.vector.reciprocal(dlast[:, k], gs[:, b, 1, :]).then_inc(gv, 1)
                        dve.wait_ge(gv, base + 5)
                        nc.vector.tensor_tensor(gs[:, b, 2, :], dlast[:, k], droot[:, k], ALU.mult).then_inc(gv, 1)
                        dve.wait_ge(gv, base + 6)
                        for r in range(GROUP):
                            tile = operand[0][:, bass.ds(k0 + r, 1), :]
                            ins = nc.vector.tensor_scalar(tile, tile, gs[:, b, 2, r:r + 1], None, ALU.mult)
                        ins.then_inc(gv, 1)
                        nc.vector.tensor_copy(near_at[:, k, :], top_at[:, b, :, 0:TOPK]).then_inc(gv, 1)

                    def rank(g, i=0):
                        for r in range(GROUP):
                            k = GROUP * g + r
                            dve.wait_ge(zz_out, 4 * (k + 1) + 8 * GROUP * i)
                            if g >= 2 and r == 0:
                                dve.wait_ge(gv, len(GV) * (g - 1) + 2 * len(GV) * i)
                            apart(dve)
                            nc.vector.max(top[:, g % 2, r, :], dist[k % 2][:, :]).then_inc(ranked, 1)
                            dve.wait_ge(ranked, 2 * k + 1 + 4 * GROUP * i)
                            apart(dve)
                            nc.vector.max_index(top_at[:, g % 2, r, :], top[:, g % 2, r, :], dist[k % 2][:, :]
                                                ).then_inc(ranked, 1)
                            if g > 0 and r == 1:
                                settle_b(g - 1, i)
                            if g > 0 and r == 3:
                                settle_c(g - 1, i)
                        settle_a(g, i)

                    rank(0)
                    rank(1)
                    with dve.Fori(0, NG // 2 - 1) as i:
                        rank(2, i)
                        rank(3, i)
                    settle_b(NG - 1, 0)
                    settle_c(NG - 1, 0)

                def split_group(g, i=0):
                    n = sx_no[s, g]
                    dve.wait_ge(sx_hi, n + 1 + (BODY // GROUP) * i)
                    nc.vector.tensor_tensor(split_x[:, n % 2, :, 1, :], operand[src][:, bass.ds(GROUP * g + BODY * i, GROUP), :],
                                            split_x[:, n % 2, :, 0, :].bitcast(F32), ALU.subtract).then_inc(sx_lo, 1)

                def lo_part(t, i=0):
                    n, n_hi = lo_no[s, t], hi_no[s, t]
                    dve.wait_ge(hi_ready, n_hi + 1 + BODY * i)
                    slot_free(dve, s, t, i, n, lo_tile, LO)
                    nc.vector.tensor_tensor(lo[:, n % LO, :], loaded(s, t), hi[:, n_hi % HI, :].bitcast(F32), ALU.subtract
                                            ).then_inc(lo_ready, 1)

                epi = Woven(None if s == LAST else epilogue(s + 1))
                for t in range(PEELED):
                    if (s, t // GROUP) in sx_no and t % GROUP == 0:
                        split_group(t // GROUP)
                    if (s, t) in lo_no:
                        lo_part(t)
                    if (s, t) in NEAR_AT:
                        sum_near(NEAR_AT[s, t])
                    epi.after(t)
                epi.finish()
                with dve.Fori(0, LOOPS) as i:
                    for t in range(PEELED, PEELED + BODY):
                        if t % GROUP == 0:
                            split_group(t // GROUP, i)
                        lo_part(t, i)
                        if (s, t) in NEAR_AT:
                            sum_near(NEAR_AT[s, t], i)
            for k in range(NK - GROUP, NK):
                sum_near(k)
            for _ in epilogue(NS + 1):
                pass

        @block.gpsimd
        def _(pool):
            nc.gpsimd.memset(pick_half[:], -0.5).then_inc(setup_g, 1)
            nc.gpsimd.memset(two_rows[:].bitcast(F32), 0.0).then_inc(setup_g, 1)
            pool.wait_ge(setup_g, 2)
            nc.gpsimd.memset(two_rows[0:1, :].bitcast(F32), 1.0).then_inc(setup_g, 1)
            nc.gpsimd.memset(two_rows[32:33, :].bitcast(F32), 1.0).then_inc(setup_g, 1)

            def stage(g, i=0):
                if g >= 2:
                    pool.wait_ge(zz_done, 4 * GROUP * (g - 1) + 8 * GROUP * i)
                cols = bass.ds(GROUP * P * g + 2 * GROUP * P * i, GROUP * P)
                for part in range(2):
                    ins = nc.gpsimd.tensor_copy(split_x[:, g % 2, :, part, :], by_tile(zT[:, part, cols].bitcast(F32)))
                ins.then_inc(z_staged, 1)

            def stage_x(i):
                pool.wait_ge(gv, len(GV) + len(GV) * i)
                pool.wait_ge(tile_done, NK * LAST + RAW * i)
                nc.gpsimd.tensor_copy(early_x[:], operand[0][:, bass.ds(RAW * i, RAW), :]).then_inc(x_staged, 1)

            pool.wait_ge(zv, 2)
            pool.wait_ge(tile_done, NK * LAST)
            stage(0)
            stage(1)
            with pool.Fori(0, NG // 2 - 1) as i:
                stage(2, i)
                stage_x(i)
                stage(3, i)

            for q in rows_out:
                pool.wait_ge(q, 16 * NG // 2)
            pool.wait_ge(gv, len(GV) * NG)
            for k in range(NK):
                if k >= GROUP:
                    pool.wait_ge(near_done, 2 * (k - GROUP + 1))
                for t in range(TOPK):
                    nc.gpsimd.indirect_dma_start(near_rows[:, k % GROUP, t, :], None, rows_dram,
                                                 bass.IndirectOffsetOnAxis(ap=near_at[:, k, t:t + 1], axis=0)
                                                 ).then_inc(fetched[k % GROUP], 16)

        @block.tensor
        def _(pe):
            steps = Steps(pe, "p")

            def epilogue(e):
                kind, half = KINDS[e], e % 2
                if kind == "none":
                    return
                when = iter(WHEN[kind]["p"])
                yield next(when)
                if kind == "last":
                    pe.wait_ge(near_done, 2 * HK * (half + 1))
                    for k in range(HK):
                        ins = nc.tensor.matmul(nat(half)[:, k, :], near_sum[:, k, :], weights["ident"][:],
                                               start=False, stop=True, skip_group_check=True)
                    steps.did(e, "near", ins)
                    yield next(when)
                wait(pe, "a", e, "yT")
                for k in range(HK):
                    ins = nc.tensor.matmul(nat(half)[:, k, :], by_tile(yT)[:, k, :], weights[WEIGHT[kind]][:],
                                           start=True, stop=True, skip_group_check=True)
                steps.did(e, "nat", ins)

            pe.wait_ge(const_in, 16 * CONSTS)
            for h in range(2):
                wait(pe, "a", 0, f"h{h}")
                for k in range(HK):
                    ins = nc.tensor.transpose(nat(h)[:, k, :], rows[:, h * HK + k, :], weights["ident"][:])
                steps.did(0, f"hT{h}", ins)
            for h in range(2):
                wait(pe, "v", 0, f"hT{h}")
                for k in range(HK):
                    ins = nc.tensor.matmul(nat(h)[:, k, :], by_tile(work[:, h, :])[:, k, :], weights["ball"][:],
                                           start=True, stop=True)
                steps.did(0, f"mx{h}", ins)

            for s, (mat, half, src, kind) in enumerate(SWEEPS):
                if s == LAST:
                    for _ in epilogue(s + 1):
                        pass
                    pe.wait_ge(setup_g, 4)
                    for h in range(2):
                        wait(pe, "v", s + h, "leaky")
                        wait(pe, "v", s + h, "z")
                        for k in range(HK):
                            ins = nc.tensor.transpose(nat(h)[:, k, :], z[:, h * HK + k, :], weights["ident"][:])
                        ins.then_inc(zp, 1)
                    for h in range(2):
                        pe.wait_ge(za, ZA.index(f"sq{h}") + 1)
                        pe.wait_ge(zv, h + 1)
                        for b in range(4):
                            ins = nc.tensor.matmul(ps[:, 4 * h + b, :], pick_half[:], work[:, h, b * BANK:(b + 1) * BANK],
                                                   start=True, stop=True)
                        ins.then_inc(zp, 1)
                    pe.wait_ge(zv, len(ZV))
                    pe.wait_ge(za, len(ZA))

                    def early(j, i):
                        r = ring_no[s, j]
                        pe.wait_ge(x_staged, 1 + i)
                        pe.wait_ge(raw_in[r % RAW], 16 * (r // RAW + 1) + 16 * i)
                        for b in range(4):
                            ins = nc.tensor.matmul(ps[:, b, :], early_x[:, j, :], raw[:, r % RAW, b * BANK:(b + 1) * BANK],
                                                   start=False, stop=True, skip_group_check=True)
                        ins.then_inc(tile_done, 1)

                    def distances(g, i=0):
                        pe.wait_ge(z_staged, g + 1 + 2 * i)
                        for r in range(GROUP):
                            k = GROUP * g + r
                            for c in range(4):
                                n = 4 * k + c
                                if n >= 2:
                                    pe.wait_ge(zz_out, n - 1 + 8 * GROUP * i)
                                for b in (2 * c, 2 * c + 1):
                                    cols, bank = slice(b * BANK, (b + 1) * BANK), ps[:, 4 + b % 4, :]
                                    z_hi, z_lo = split_x[:, g % 2, r, 0, :], split_x[:, g % 2, r, 1, :]
                                    nc.tensor.matmul(bank, two_rows[:], sq_row[:, cols], start=True, stop=False)
                                    nc.tensor.matmul(bank, z_lo, zT[:, 0, cols], start=False, stop=False)
                                    nc.tensor.matmul(bank, z_hi, zT[:, 1, cols], start=False, stop=False)
                                    ins = nc.tensor.matmul(bank, z_hi, zT[:, 0, cols], start=False, stop=True)
                                ins.then_inc(zz_done, 1)
                            if g >= 2 and r % 2 == 1:
                                early(r // 2 + 2 * (g % 2), i)

                    distances(0)
                    distances(1)
                    with pe.Fori(0, NG // 2 - 1) as i:
                        distances(2, i)
                        distances(3, i)

                if s < 2:
                    wait(pe, "v", 0, f"moved{s}")
                elif s > LAST:
                    pe.wait_ge(zz_out, 4 * NK)
                elif s < LAST:
                    who, name = PSUM_READ[KINDS[s]]
                    wait(pe, who, s, name)

                def products(t, i=0):
                    if t in WHOLE[s]:
                        wait_operand(pe, s, t // HK)
                        wait_tile(pe, s, t)
                        if s in SUMMED:
                            pe.wait_ge(hi_ready, hi_no[s, t] + 1)
                        parts = ((operand[src][:, t, :], loaded(s, t)),)
                    else:
                        n = sx_no[s, t // GROUP]
                        pe.wait_ge(sx_lo, n + 1 + (BODY // GROUP) * i)
                        pe.wait_ge(hi_ready, hi_no[s, t] + 1 + BODY * i)
                        pe.wait_ge(lo_ready, lo_no[s, t] + 1 + BODY * i)
                        x_hi, x_lo = split_x[:, n % 2, t % GROUP, 0, :], split_x[:, n % 2, t % GROUP, 1, :]
                        tile_hi, tile_lo = hi[:, hi_no[s, t] % HI, :], lo[:, lo_no[s, t] % LO, :]
                        parts = ((x_hi, tile_lo), (x_hi, tile_hi), (x_lo, tile_hi))
                    for j, (w, tile) in enumerate(parts):
                        for b in range(4):
                            ins = nc.tensor.matmul(ps[:, 4 * half + b, :], w, tile[:, b * BANK:(b + 1) * BANK],
                                                   start=(t == 0 and j == 0), stop=True, skip_group_check=True)
                    ins.then_inc(tile_done, 1)

                epi = Woven(None if s == LAST else epilogue(s + 1))
                for t in range(EARLY if s == LAST else 0, PEELED):
                    products(t)
                    epi.after(t)
                epi.finish()
                with pe.Fori(0, LOOPS) as i:
                    for t in range(PEELED, PEELED + BODY):
                        products(t, i)
            for _ in epilogue(NS + 1):
                pass


def kernel(x, adj, L0_gnn_weight, L0_gnn_bias, L1_gnn_W, L1_gnn_b, L2_gnn_W_in, L2_gnn_W_out,
           L3_gnn_W1, L3_gnn_b1, L3_gnn_W2, L3_gnn_b2):
    import concourse.bacc as bacc
    from concourse.bass_utils import run_bass_kernel_spmd

    arrays = {
        "x": x, "adj": adj, "adj_t": np.asarray(adj).T, "w_ball_t": np.asarray(L0_gnn_weight).T,
        "b_ball": L0_gnn_bias, "w_swish": L1_gnn_W, "b_swish": L1_gnn_b, "w_in": L2_gnn_W_in,
        "w_out": L2_gnn_W_out, "w_embed": L3_gnn_W1, "b_embed": L3_gnn_b1, "w_last": L3_gnn_W2,
        "b_last": L3_gnn_b2, "eye": np.eye(P, dtype=np.float32)}
    arrays = {n: np.ascontiguousarray(a) for n, a in arrays.items()}
    nc = bacc.Bacc("TRN2", target_bir_lowering=False, num_devices=1)
    args = [nc.dram_tensor(n, a.shape, F32, kind="ExternalInput").ap() for n, a in arrays.items()]
    rows_dram = nc.dram_tensor("rows", (N, P), F32, kind="Internal").ap()
    out = nc.dram_tensor("out", (N, P), F32, kind="ExternalOutput").ap()
    graph_layers(nc, *args, rows_dram, out)
    r = run_bass_kernel_spmd(nc, [arrays], core_ids=[0])
    return r.results[0]["out"]
```

```python
from contextlib import ExitStack
from itertools import repeat

import numpy as np

import concourse.bass as bass
from concourse import mybir
from concourse.alu_op_type import AluOpType as ALU

F32 = mybir.dt.float32
F32R = mybir.dt.float32r
U32 = mybir.dt.uint32
ACT = mybir.ActivationFunctionType
AX_X = mybir.AxisListType.X

P = 128
N = 4096
NK = N // P
HALF = N // 2
HK = NK // 2
BANK = 512
GROUP = 4
NG = NK // GROUP
BODY = 8
PEELED = 16
LOOPS = (NK - PEELED) // BODY
EARLY = 12
AHEAD_HI, AHEAD_LO = 4, 2
RAW, HI, LO = 4, 4, 2
KEPT = ((4, 9, 14), (4, 9))
QUARTER = HK // 4
TOPK = 4

MIN_NORM = 1e-15
MAX_NORM = float(np.float32(1.0) - np.float32(0.004))
CLIP = float(np.float32(1.0 - 1e-7))
ARTANH_MAX_NORM = float(np.arctanh(MAX_NORM))
LN_EPS = 1e-5
DIST_EPS = 1e-10

SWEEPS = [("T", 0, 0, "ball"), ("T", 1, 0, "ball"),
          ("T", 0, 1, "swish"), ("T", 1, 1, "swish"),
          ("T", 0, 0, "swish_norm"), ("T", 1, 0, "swish_norm"),
          ("A", 0, 1, "columns"), ("A", 1, 1, "columns"),
          ("T", 0, 1, "rows"), ("T", 1, 1, "rows"),
          ("T", 0, 0, "embed"), ("T", 1, 0, "embed"),
          ("T", 0, 0, "last"), ("T", 1, 0, "last")]
NS = len(SWEEPS)
LAST = NS - 2
SUMMED = (0, 1, 6, 7)
WHOLE = [(), (1, 8, 9, 10), (7, 10), (4,), (), (4, 7), (4,),
         (), (4,), (4, 7, 9), (5, 9), (2, 4), range(PEELED), (3, 4, 7, 9)]
for _s in range(NS):
    assert _s == LAST or all(t < PEELED - RAW - 1 for t in WHOLE[_s])

KINDS = ["enter", "none"] + [s[3] for s in SWEEPS]
WEIGHT = {"ball": "ident", "swish": "swish", "swish_norm": "swish", "columns": "out",
          "rows": "in", "embed": "embed", "last": "last"}

YT, NAT, NEAR = ([f"{n}{q}" for q in range(4)] for n in ("yT", "nat", "near"))
NORM_V = ["stats", "diff", "msum", "vsum", "dsq", "var", "vareps", "rstd", "shift"]
ARTANH_V = ["plus", "minus", "inv", "ratio", "sq", "p1", "p2", "p3", "p4", "small", "gap", "pick", "artanh"]

STEPS = {
    "enter": {
        "v": [n + "0" for n in NORM_V] + [n + "1" for n in NORM_V]
        + [f"{n}{h}" for h in range(2) for n in ("hT_0", "hT_1", "hT_2", "hT_3", "hh", "hh_sum")] + ["mb0", "mb_sum0", "mb1", "mb_sum1", "floor", "h_clip"]
        + ["h_" + n for n in ARTANH_V]
        + ["hn_inv", "arg", "arg2", "cap", "mx_inv", "q", "q_sq", "x2", "xy", "xy1", "top", "left", "x2y2",
           "den", "den_floor", "den_inv", "top_q", "a", "c", "ax2", "cxy", "m_half", "m_part", "cc", "m_sum",
           "m_guard", "m_floor", "m_clip"]
        + ["m_" + n for n in ARTANH_V] + ["m_inv2", "m_scale", "a_out", "c_out", "out0", "out1"],
        "a": ["std0", "h_00", "h_10", "h_20", "h_30", "std1", "h_01", "h_11", "h_21", "h_31",
              "mx_sq0", "mx_sq1", "norms", "h_ln", "tanh", "m_norm", "m_ln", "cb0", "cb1"],
        "p": [f"{n}_{q}{h}" for h in range(2) for n in ("hT", "mx") for q in range(4)]},
    "none": {"v": [], "a": [], "p": []},
    "ball": {
        "v": ["s_sum", "relu_sum", "s_floor", "s_inv", "s_scale", "u_norm", "u_floor", "u_inv", "u_scale",
              "scale", "res"] + NORM_V,
        "a": YT + ["s_sq", "relu", "relu_sq", "norms", "u_tanh", "std", "out"], "p": NAT},
    "swish": {"v": ["biased"], "a": YT + ["out"], "p": NAT},
    "swish_norm": {"v": ["biased", "res"] + NORM_V, "a": YT + ["swish", "std", "out"], "p": NAT},
    "columns": {"v": ["sum", "pos", "masked", "one", "safe", "inv", "res"], "a": YT, "p": NAT},
    "rows": {"v": ["sum", "pos", "masked", "one", "safe", "inv", "dinv", "res"] + NORM_V
             + ["rstd_d", "shift_d"],
             "a": YT + ["droot", "std", "out"], "p": NAT},
    "embed": {"v": ["z0", "leaky0", "z1", "leaky1", "z2", "leaky2", "z3", "leaky3"], "a": YT + ["z_sq"], "p": NAT},
    "last": {"v": ["biased", "out0", "out1", "out2", "out3"], "a": YT, "p": NEAR + NAT},
}
PSUM_READ = {"ball": ("v", "relu_sum"), "swish": ("v", "biased"),
             "swish_norm": ("v", "biased"), "columns": ("v", "res"), "rows": ("v", "res"),
             "embed": ("v", "z3"), "last": ("v", "out3")}
OPERAND = {"ball": ("a", "out"), "swish": ("a", "out"),
           "swish_norm": ("a", "out"), "rows": ("a", "out")}
OPERAND_OF = {2: 0, 4: 2, 6: 4, 8: 4, 10: 8}

WHEN = {
    ("ball", 0): {"a": [1, 3, 4, 5, 8, 9, 12, 12, 13, 14, 14],
                  "v": [3, 5, 8, 8, 9, 9, 9, 10, 10, 10, 10, 10, 10],
                  "p": [0]},
    ("ball", 1): {"a": [1, 3, 4, 5, 8, 9, 13, 13, 13, 15, 15],
                  "v": [3, 5, 8, 9, 10, 10, 10, 10, 10, 10, 10, 10, 11],
                  "p": [1]},
    ("swish", 0): {"a": [1, 3], "v": [2], "p": [0]},
    ("swish", 1): {"a": [1, 5], "v": [2], "p": [0]},
    ("swish_norm", 0): {"a": [1, 3, 9, 11, 12, 13, 14],
                        "v": [2, 3, 6, 6, 6, 6, 9],
                        "p": [0]},
    ("swish_norm", 1): {"a": [1, 3, 9, 11, 12, 13, 14],
                        "v": [2, 3, 6, 6, 6, 7, 9],
                        "p": [0]},
    ("columns", 0): {"a": [1], "v": [2, 3, 4, 5, 6], "p": [0]},
    ("columns", 1): {"a": [1], "v": [2, 2, 3, 4, 5], "p": [0]},
    ("rows", 0): {"a": [1, 3, 11, 13, 14, 14, 15],
                  "v": [2, 3, 3, 4, 5, 6, 7, 7, 8, 9, 9],
                  "p": [0]},
    ("rows", 1): {"a": [1, 3, 10, 12, 13, 13, 15],
                  "v": [2, 2, 2, 4, 4, 5, 6, 6, 7, 8, 8],
                  "p": [0]},
    ("embed", 0): {"a": [1, 7, 8, 9, 10],
                   "v": [1, 4, 5, 5],
                   "p": [0]},
    ("embed", 1): {"a": [1, 7, 8, 9, 10],
                   "v": [1, 4, 5, 5],
                   "p": [0]},
    ("last", 0): {"a": [10],
                  "v": [8, 13, 13, 13, 13],
                  "p": [8, 11]},
    ("last", 1): {"a": [10],
                  "v": [8, 13, 13, 13, 13],
                  "p": [8, 11]},
}

BEHIND = [range(PEELED + 1, PEELED + BODY, 2), (0, 1, 2, 3, 4, 5, 6, 8, 10, 11, 12, 13, 14, 15),
          range(PEELED + 1, PEELED + BODY, 2)]
NEAR_AT = {(LAST, t): k for k, t in enumerate(BEHIND[0])}
NEAR_AT.update({(LAST + 1, t): LOOPS * GROUP + k for k, t in enumerate(BEHIND[1])})
NEAR_AT.update({(LAST + 1, t): LOOPS * GROUP + len(BEHIND[1]) + k for k, t in enumerate(BEHIND[2])})
NEAR_LEFT = NK - 2 * LOOPS * GROUP - len(BEHIND[1])

GV = ["neg", "eps", "sum", "total", "dlast", "scale", "operand", "places"]
GA = ["dist", "weight", "root"]
ZP = ["zT0", "zT1", "sq0", "sq1"]
ZA = ["hi0", "sq0", "hi1", "sq1", "row0", "row1"]
ZV = ["lo0", "lo1", "row0", "row1", "neg", "zero"]


def step_counts():
    at = {}
    for who in "vap":
        n = 0
        for e, kind in enumerate(KINDS):
            at[who, e, "begin"] = n
            for name in STEPS[kind][who]:
                n += 1
                at[who, e, name] = n
            at[who, e, "end"] = n
    return at


def graph_layers(nc, x, adj, adj_t, w_ball_t, b_ball, w_swish, b_swish, w_in, w_out, w_embed, b_embed,
                 w_last, b_last, eye, rows_dram, out):
    at = step_counts()

    ring_no, tile_at = {}, []
    for s, (mat, half, _, _) in enumerate(SWEEPS):
        for t in range(NK):
            if not (mat == "T" and t in KEPT[half]) or s == LAST:
                ring_no[s, t] = len(tile_at)
                tile_at.append(NK * s + t)

    hi_no, lo_no, sx_no, hi_tile, lo_tile, sx_end = {}, {}, {}, [], [], []
    for s in range(NS):
        for t in range(NK):
            if s in SUMMED or t not in WHOLE[s]:
                hi_no[s, t] = len(hi_tile)
                hi_tile.append(NK * s + t)
            if t not in WHOLE[s]:
                lo_no[s, t] = len(lo_tile)
                lo_tile.append(NK * s + t)
            if t % GROUP == 0 and any(u not in WHOLE[s] for u in range(t, t + GROUP)):
                sx_no[s, t // GROUP] = len(sx_end)
                sx_end.append(NK * s + t + GROUP)

    with ExitStack() as ctx:
        def sb(name, shape, dt=F32):
            return ctx.enter_context(nc.sbuf_tensor(name, shape, dt))

        def sem(name):
            return ctx.enter_context(nc.semaphore(name))

        raw = sb("raw", [P, RAW, HALF])
        kept_tiles = {(h, t): sb(f"kept{h}_{t}", [P, HALF]) for h in range(2) for t in KEPT[h]}
        hi = sb("hi", [P, HI, HALF], F32R)
        lo = sb("lo", [P, LO, HALF], F32R)
        operand = [sb("operand0", [P, NK, P]), sb("operand1", [P, NK, P])]
        res = sb("res", [P, NK, P])
        work = sb("work", [P, 2, HALF])
        yT, scr = work[:, 0, :], work[:, 1, :]
        split_x = sb("split_x", [P, 2, GROUP, 2, P], F32R)
        weights = {n: sb("weight_" + n, [P, P]) for n in ("ident", "ball", "swish", "in", "out", "embed", "last")}
        bias = {n: sb("bias_" + n, [P, P]) for n in ("swish", "embed", "last")}
        ball_bias = sb("ball_bias", [P, P])
        bias["ball"] = ball_bias
        bb = sb("bb", [P, 8])
        stats = sb("stats", [P, NK, 6])
        SMALL = 37
        sm = sb("sm", [P, SMALL, NK])
        col_part = sb("col_part", [P, 2, NK])
        row_part = sb("row_part", [P, 2, NK])
        deg, pos, one, inv_sum = (sb(n, [P, NK]) for n in ("deg", "pos", "one", "inv_sum"))
        droot, dinv = sb("droot", [P, NK]), sb("dinv", [P, NK])
        z_sq = sb("z_sq", [P, NK])
        neg_sq = sb("neg_sq", [P, NK])
        pick_half = sb("pick_half", [P, P])
        two_rows = sb("two_rows", [P, P], F32R)
        top = sb("top", [P, 2, GROUP, 8])
        top_at = sb("top_at", [P, 2, GROUP, 8], U32)
        near_at = sb("near_at", [P, NK, TOPK], U32)
        near_w = sb("near_w", [P, NK, TOPK])
        gd = sb("gd", [P, 2, GROUP, TOPK])
        gs = sb("gs", [P, 2, 3, GROUP])
        dlast = sb("dlast", [P, NK])
        z = operand[1]
        zT = hi[:, :, :].rearrange("p (a b) n -> p a (b n)", a=2)
        sq_row = lo[:, :, :].rearrange("p a n -> p (a n)")
        dist = [operand[1][:, :, :].rearrange("p k f -> p (k f)"),
                work[:, :, :].rearrange("p a n -> p (a n)")]
        rows = operand[1]
        early_x = sm[:, 0:RAW * P // NK, :].rearrange("p (r a) b -> p r (a b)", r=RAW)
        near_rows = operand[1][:, 0:HK, :].rearrange("p (r t) f -> p r t f", t=TOPK)
        near_sum = operand[1][:, HK:NK, :]

        ps = ctx.enter_context(nc.psum_tensor("ps", [P, 8, BANK], F32))

        def by_tile(ap):
            return ap.rearrange("p (k f) -> p k f", f=P)

        def flat(ap):
            return ap.rearrange("p k f -> p (k f)")

        def acc(half):
            return flat(ps[:, 4 * half:4 * half + 4, :])

        def nat(half):
            return by_tile(acc(half))

        BANKS = [slice(q * BANK, (q + 1) * BANK) for q in range(4)]

        def half_of(buf, half):
            return buf[:, half * HK:(half + 1) * HK]

        def per_node(v):
            return v.unsqueeze(2).broadcast_to([P, HK, P])

        def per_feature(v):
            return v[:, :].unsqueeze(1).broadcast_to([P, HK, P])

        def sink(i):
            return hi[:, i, :]

        def flat2(buf):
            return buf[:, :, :].rearrange("p a n -> p (a n)")

        raw_in = [sem(f"raw_in{i}") for i in range(RAW)]
        kept_in = {at: sem(f"kept_in{at[0]}_{at[1]}") for at in kept_tiles}
        x_in = [sem("x_in0"), sem("x_in1")]
        const_in = sem("const_in")
        CONSTS = 11
        hi_ready = sem("hi_ready")
        lo_ready = sem("lo_ready")
        tile_done = sem("tile_done")
        sx_hi, sx_lo = sem("sx_hi"), sem("sx_lo")
        step = {"v": sem("v_step"), "a": sem("a_step"), "p": sem("p_step")}
        setup_v, setup_a, setup_g = sem("setup_v"), sem("setup_a"), sem("setup_g")
        zp, za, zv = sem("zp"), sem("za"), sem("zv")
        x_staged = sem("x_staged")
        z_staged = sem("z_staged")
        zz_done = sem("zz_done")
        zz_out = sem("zz_out")
        ranked = sem("ranked")
        gv, ga = sem("gv"), sem("ga")
        rows_out = [sem("rows_out0"), sem("rows_out1")]
        fetched = [sem(f"fetched{i}") for i in range(GROUP)]
        near_scaled = sem("near_scaled")
        near_done = sem("near_done")
        done_out = [sem(f"done_out{q}") for q in range(4)]
        waited = sem("waited")

        block = ctx.enter_context(nc.Block())

        def wait(eng, who, e, name):
            if at[who, e, name] > 0:
                eng.wait_ge(step[who], at[who, e, name])

        class Steps:

            def __init__(self, eng, who):
                self.eng, self.who, self.count = eng, who, 0

            def did(self, e, name, ins):
                assert at[self.who, e, name] == self.count + 1, (KINDS[e], name)
                self.count += 1
                ins.then_inc(step[self.who], 1)

            def own(self):
                self.eng.wait_ge(step[self.who], self.count)

        class Woven:

            def __init__(self, steps):
                self.steps, self.behind = steps, 0
                if steps is not None:
                    self.behind = next(steps, None)

            def after(self, t):
                while self.behind is not None and self.steps is not None and self.behind <= t:
                    self.behind = next(self.steps, None)

            def finish(self):
                self.after(NK)

        def apart(eng):
            eng.sem_inc(waited)

        def wait_operand(eng, s, g, i=0):
            if s >= LAST:
                eng.wait_ge(gv, len(GV) * (g + 1) + 2 * len(GV) * i)
                return
            half = g // (NG // 2)
            if s < 2:
                wait(eng, "v", 0, f"out{half}")
                return
            e = OPERAND_OF[s - s % 2] + half + 2
            who, name = OPERAND[KINDS[e]]
            wait(eng, who, e, name)

        def wait_tile(eng, s, t, i=0):
            if (s, t) not in ring_no:
                eng.wait_ge(kept_in[SWEEPS[s][1], t], 16)
            else:
                r = ring_no[s, t]
                eng.wait_ge(raw_in[r % RAW], 16 * (r // RAW + 1) + 16 * (BODY // RAW) * i)

        def loaded(s, t):
            if (s, t) not in ring_no:
                return kept_tiles[SWEEPS[s][1], t][:, :]
            return raw[:, ring_no[s, t] % RAW, :]

        def slot_free(eng, s, t, i, no, tiles, depth):
            if no >= depth:
                before = tiles[no - depth] if t < PEELED else NK * s + t - depth
                eng.wait_ge(tile_done, before + 1 + BODY * i)

        @block.sync
        def _(sp):
            for h in range(2):
                sp.dma_start(half_of(res, h), half_of(x.rearrange("(k p) f -> p k f", p=P), h)).then_inc(x_in[h], 16)
            for name, src in (("ident", eye), ("ball", w_ball_t), ("swish", w_swish), ("in", w_in),
                              ("out", w_out), ("embed", w_embed), ("last", w_last)):
                sp.dma_start(weights[name][:], src).then_inc(const_in, 16)
            for name, src in (("ball", b_ball), ("swish", b_swish), ("embed", b_embed), ("last", b_last)):
                sp.dma_start(bias[name][:], src.rearrange("(a f) -> a f", a=1).broadcast_to([P, P])
                             ).then_inc(const_in, 16)

            rows_view = rows_dram.rearrange("(k p) f -> p k f", p=P)

            def store_rows(g, i=0):
                sp.wait_ge(gv, len(GV) * g + GV.index("operand") + 1 + 2 * len(GV) * i)
                apart(sp)
                if g >= 2:
                    sp.wait_ge(rows_out[g % 2], 16 * (g // 2) + 16 * i)
                apart(sp)
                k = bass.ds(GROUP * g + 2 * GROUP * i, GROUP)
                sp.dma_start(rows_view[:, k, :], operand[0][:, k, :]).then_inc(rows_out[g % 2], 16)

            for s, (mat, half, _, _) in enumerate(SWEEPS):
                src = {"T": adj_t, "A": adj}[mat]

                def load(t, i=0):
                    r = ring_no[s, t]
                    if r >= RAW:
                        before = tile_at[r - RAW] if t < PEELED else NK * s + t - RAW
                        s_, t_ = before // NK, before % NK
                        if t_ in WHOLE[s_] or (s == LAST and t >= PEELED):
                            sp.wait_ge(tile_done, before + 1 + BODY * i)
                        else:
                            sp.wait_ge(lo_ready, lo_no[s_, t_] + 1 + BODY * i)
                    sp.dma_start(raw[:, r % RAW, :],
                                 src[bass.ds((t + BODY * i) * P, P), half * HALF:(half + 1) * HALF]
                                 ).then_inc(raw_in[r % RAW], 16)

                if s == LAST:
                    def load_next(j, i):
                        sp.wait_ge(tile_done, NK * s + j + 1 + RAW * i)
                        r = ring_no[s, j]
                        sp.dma_start(raw[:, r % RAW, :],
                                     src[bass.ds((RAW + j + RAW * i) * P, P), half * HALF:(half + 1) * HALF]
                                     ).then_inc(raw_in[r % RAW], 16)

                    sp.wait_ge(zp, len(ZP))
                    for t in range(RAW):
                        load(t)
                    store_rows(0)
                    store_rows(1)
                    with sp.Fori(0, NG // 2 - 1) as i:
                        load_next(0, i)
                        load_next(1, i)
                        store_rows(2, i)
                        load_next(2, i)
                        load_next(3, i)
                        store_rows(3, i)
                else:
                    for t in range(PEELED):
                        if (s, t) in ring_no:
                            load(t)
                        elif s < 2:
                            sp.dma_start(kept_tiles[half, t][:, :],
                                         src[t * P:(t + 1) * P, half * HALF:(half + 1) * HALF]
                                         ).then_inc(kept_in[half, t], 16)
                with sp.Fori(0, LOOPS) as i:
                    for t in range(PEELED, PEELED + BODY):
                        load(t, i)

            for h in range(2):
                for q in range(4):
                    wait(sp, "v", NS + h, f"out{q}")
                    if h > 0:
                        sp.wait_ge(done_out[q], 16)
                    tiles = slice(h * HK + q * QUARTER, h * HK + (q + 1) * QUARTER)
                    sp.dma_start(out.rearrange("(k p) f -> p k f", p=P)[:, tiles, :], res[:, tiles, :]
                                 ).then_inc(done_out[q], 16)
            for q in range(4):
                sp.wait_ge(done_out[q], 32)

        @block.scalar
        def _(act):
            steps = Steps(act, "a")
            did = steps.did

            def v(i):
                return sm[:, i, 0:HK]

            def w(i):
                return sm[:, i, :]

            def begin(e):
                for who in "vp":
                    wait(act, who, e, "begin")
                if e > 0:
                    steps.own()

            def normalise(e, dst, name, when):
                yield next(when)
                wait(act, "v", e, "vareps")
                did(e, "std", nc.scalar.activation(v(6), v(5), ACT.Sqrt))
                for k in range(HK):
                    if k % QUARTER == 0:
                        yield next(when)
                    if k == 0:
                        wait(act, "v", e, "shift_d" if KINDS[e] == "rows" else "shift")
                    ins = nc.scalar.activation(dst[:, k, :], res[:, e % 2 * HK + k, :], ACT.Relu,
                                               scale=sm[:, 7, k:k + 1], bias=sm[:, 8, k:k + 1])
                did(e, name, ins)

            def square_sums(e, name, dst, src, sums, when=None, ready=None):
                for k in range(HK):
                    if when is not None and k % QUARTER == 0:
                        yield next(when)
                    if ready is not None and k % QUARTER == 0:
                        ready(k // QUARTER)
                    ins = nc.scalar.activation(dst[:, k, :], src[:, k, :], ACT.Square, accum_out=sums[:, k:k + 1])
                did(e, name, ins)
                steps.own()

            def epilogue(e):
                kind, half = KINDS[e], e % 2
                if kind == "none":
                    return
                when = iter(WHEN[kind, half]["a"])
                yield next(when)
                begin(e)
                act.wait_ge(tile_done, NK * (e - 1))
                for q, cols in enumerate(BANKS):
                    if kind == "last":
                        wait(act, "p", e, f"near{q}")
                    did(e, f"yT{q}", nc.scalar.copy(yT[:, cols], acc(half)[:, cols]))
                if kind == "ball":
                    yield next(when)
                    wait(act, "p", e, "nat3")
                    did(e, "s_sq", nc.scalar.activation(scr, acc(half), ACT.Square))
                    yield next(when)
                    did(e, "relu", nc.scalar.activation(yT, acc(half), ACT.Relu))
                    steps.own()
                    yield next(when)
                    did(e, "relu_sq", nc.scalar.activation(acc(half), yT, ACT.Square))
                    yield next(when)
                    wait(act, "v", e, "relu_sum")
                    did(e, "norms", nc.scalar.activation(sm[:, 11:13, :], sm[:, 9:11, :], ACT.Sqrt))
                    yield next(when)
                    wait(act, "v", e, "u_floor")
                    did(e, "u_tanh", nc.scalar.activation(v(16), v(15), ACT.Tanh))
                elif kind in ("swish", "swish_norm"):
                    yield next(when)
                    wait(act, "v", e, "biased")
                    if kind == "swish":
                        did(e, "out", nc.scalar.activation(half_of(operand[0], half), by_tile(scr), ACT.Silu))
                    else:
                        did(e, "swish", nc.scalar.activation(yT, scr, ACT.Silu))
                elif kind == "rows":
                    yield next(when)
                    wait(act, "v", e, "sum")
                    did(e, "droot", nc.scalar.activation(droot[:], deg[:], ACT.Sqrt))
                elif kind == "embed":
                    yield from square_sums(e, "z_sq", by_tile(yT), half_of(z, half), half_of(z_sq, half), when,
                                           lambda q: wait(act, "v", e, f"leaky{q}"))
                if kind in ("ball", "swish_norm", "rows"):
                    dst = operand[0 if kind == "rows" else 1]
                    yield from normalise(e, half_of(dst, half), "out", when)

            def hi_part(s, t, i=0):
                mat, half, _, _ = SWEEPS[s]
                n, tile = hi_no[s, t], loaded(s, t)
                wait_tile(act, s, t, i)
                slot_free(act, s, t, i, n, hi_tile, HI)
                if s in SUMMED:
                    sums = {"T": col_part, "A": row_part}[mat]
                    nc.scalar.activation(hi[:, n % HI, :], tile, ACT.Identity,
                                         accum_out=sums[:, half, bass.ds(t + BODY * i, 1)]).then_inc(hi_ready, 1)
                else:
                    nc.scalar.copy(hi[:, n % HI, :], tile).then_inc(hi_ready, 1)

            def bias_point():
                act.wait_ge(const_in, 16 * CONSTS)
                nc.scalar.activation(sink(2)[:, 0:P], ball_bias[:], ACT.Square, accum_out=bb[:, 0:1]).then_inc(setup_a, 1)
                act.wait_ge(setup_a, 1)
                nc.scalar.activation(bb[:, 1:2], bb[:, 0:1], ACT.Sqrt).then_inc(setup_a, 1)
                act.wait_ge(setup_v, 1)
                nc.scalar.activation(bb[:, 3:4], bb[:, 2:3], ACT.Tanh).then_inc(setup_a, 1)
                act.wait_ge(setup_v, 4)
                nc.scalar.activation(sink(3)[:, 0:P], ball_bias[:], ACT.Square, accum_out=bb[:, 6:7]).then_inc(setup_a, 1)
                act.wait_ge(setup_a, 4)

            def enter():
                for h in range(2):
                    wait(act, "v", 0, f"vareps{h}")
                    did(0, f"std{h}", nc.scalar.activation(half_of(w(6), h), half_of(w(5), h), ACT.Sqrt))
                    wait(act, "v", 0, f"shift{h}")
                    for k in range(h * HK, (h + 1) * HK):
                        ins = nc.scalar.activation(rows[:, k, :], res[:, k, :], ACT.Relu,
                                                   scale=sm[:, 7, k:k + 1], bias=sm[:, 8, k:k + 1])
                        if k % QUARTER == QUARTER - 1:
                            did(0, f"h_{k % HK // QUARTER}{h}", ins)
                steps.own()
                for h in range(2):
                    if h == 1:
                        bias_point()
                    for _ in square_sums(0, f"mx_sq{h}", by_tile(sink(h)), nat(h), half_of(w(10), h), repeat(0),
                                         lambda q: wait(act, "p", 0, f"mx_{q}{h}")):
                        pass
                wait(act, "v", 0, "hh_sum1")
                did(0, "norms", nc.scalar.activation(sm[:, 11:13, :], sm[:, 9:11, :], ACT.Sqrt))
                wait(act, "v", 0, "h_ratio")
                did(0, "h_ln", nc.scalar.activation(w(19), w(18), ACT.Ln))
                wait(act, "v", 0, "arg2")
                did(0, "tanh", nc.scalar.activation(w(27), w(26), ACT.Tanh))
                hi_part(0, 0)
                hi_part(0, 1)
                wait(act, "v", 0, "m_guard")
                did(0, "m_norm", nc.scalar.activation(w(11), w(9), ACT.Sqrt))
                wait(act, "v", 0, "m_ratio")
                did(0, "m_ln", nc.scalar.activation(w(19), w(18), ACT.Ln))
                wait(act, "v", 0, "c_out")
                for h in range(2):
                    for k in range(h * HK, (h + 1) * HK):
                        ins = nc.scalar.activation(by_tile(flat2(work))[:, k, :], ball_bias[:], ACT.Copy,
                                                   scale=sm[:, 32, k:k + 1])
                    did(0, f"cb{h}", ins)
                hi_part(0, 2)
                hi_part(0, 3)

            enter()

            def scale_near(k, i=0):
                r = k % GROUP
                act.wait_ge(fetched[r], 16 * TOPK * (k // GROUP + 1) + 16 * TOPK * i)
                apart(act)
                for t in range(TOPK):
                    ins = nc.scalar.activation(near_rows[:, r, t, :], near_rows[:, r, t, :], ACT.Copy,
                                               scale=near_w[:, bass.ds(k + GROUP * i, 1), t])
                ins.then_inc(near_scaled, 1)

            for s, (mat, half, src, kind) in enumerate(SWEEPS):
                if s == LAST:
                    def make_zT(h):
                        act.wait_ge(zp, ZP.index(f"zT{h}") + 1)
                        if h == 0:
                            act.wait_ge(tile_done, NK * s)
                        nc.scalar.copy(zT[:, 0, h * HALF:(h + 1) * HALF], acc(h)).then_inc(za, 1)
                        nc.scalar.activation(raw[:, h, :], acc(h), ACT.Square).then_inc(za, 1)

                    tail = epilogue(s + 1)
                    next(tail)
                    next(tail)
                    make_zT(0)
                    make_zT(1)
                    for _ in tail:
                        pass
                    for h in range(2):
                        act.wait_ge(zp, ZP.index(f"sq{h}") + 1)
                        nc.scalar.copy(sq_row[:, h * HALF:(h + 1) * HALF], acc(h)).then_inc(za, 1)

                    def weigh(g, i):
                        act.wait_ge(gv, len(GV) * g + GV.index("eps") + 1 + 2 * len(GV) * i)
                        nc.scalar.activation(gd[:, g % 2, :, :], gd[:, g % 2, :, :], ACT.Sqrt).then_inc(ga, 1)
                        act.wait_ge(ga, len(GA) * g + 1 + 2 * len(GA) * i)
                        k = bass.ds(GROUP * g + 2 * GROUP * i, GROUP)
                        nc.scalar.activation(near_w[:, k, :], gd[:, g % 2, :, :], ACT.Exp, scale=-0.5).then_inc(ga, 1)

                    def root(g, i):
                        act.wait_ge(gv, len(GV) * g + GV.index("total") + 1 + 2 * len(GV) * i)
                        nc.scalar.activation(gs[:, g % 2, 1, :], gs[:, g % 2, 0, :], ACT.Sqrt).then_inc(ga, 1)

                    def leave(g, i=0):
                        for r in range(GROUP):
                            k = GROUP * g + r
                            for c in range(4):
                                act.wait_ge(zz_done, 4 * k + c + 1 + 8 * GROUP * i)
                                if c == 0 and k >= 2:
                                    act.wait_ge(ranked, 2 * (k - 1) + 4 * GROUP * i)
                                apart(act)
                                nc.scalar.activation(dist[k % 2][:, c * 2 * BANK:(c + 1) * 2 * BANK],
                                                     ps[:, 4 + c % 2 * 2:6 + c % 2 * 2, :].rearrange("p b n -> p (b n)"),
                                                     ACT.Identity, bias=neg_sq[:, bass.ds(k + 2 * GROUP * i, 1)],
                                                     scale=2.0).then_inc(zz_out, 1)
                            if g > 0 and r == 0:
                                weigh(g - 1, i)
                            if g > 0 and r == 2:
                                root(g - 1, i)

                    act.wait_ge(zv, ZV.index("neg") + 1)
                    act.wait_ge(zp, len(ZP))
                    leave(0)
                    leave(1)
                    with act.Fori(0, NG // 2 - 1) as i:
                        leave(2, i)
                        leave(3, i)
                    weigh(NG - 1, 0)
                    root(NG - 1, 0)

                def split_group(g, i=0):
                    if GROUP * g < PEELED or s == LAST:
                        wait_operand(act, s, g, i)
                    n = sx_no[s, g]
                    if n >= 2:
                        before = sx_end[n - 2] if GROUP * g < PEELED else NK * s + GROUP * (g - 1)
                        act.wait_ge(tile_done, before + BODY * i)
                    nc.scalar.copy(split_x[:, n % 2, :, 0, :], operand[src][:, bass.ds(GROUP * g + BODY * i, GROUP), :]
                                   ).then_inc(sx_hi, 1)

                if s == LAST:
                    act.wait_ge(zz_done, 4 * NK)
                epi = Woven(None if s == LAST else epilogue(s + 1))
                for t in range(PEELED):
                    if (s, t // GROUP) in sx_no and t % GROUP == 0:
                        split_group(t // GROUP)
                    if (s, t) in hi_no and hi_no[s, t] >= AHEAD_HI:
                        hi_part(s, t)
                    if (s, t) in NEAR_AT:
                        scale_near(NEAR_AT[s, t])
                    epi.after(t)
                epi.finish()
                if s != LAST:
                    wait_operand(act, s, NG - 1)
                with act.Fori(0, LOOPS) as i:
                    for t in range(PEELED, PEELED + BODY):
                        if t % GROUP == 0:
                            split_group(t // GROUP, i)
                        hi_part(s, t, i)
                        if (s, t) in NEAR_AT:
                            scale_near(NEAR_AT[s, t], i)
            for k in range(NK - NEAR_LEFT, NK):
                scale_near(k)
            for _ in epilogue(NS + 1):
                pass

        @block.vector
        def _(dve):
            steps = Steps(dve, "v")

            def v(i):
                return sm[:, i, 0:HK]

            def w(i):
                return sm[:, i, :]

            def did(e, name, ins):
                steps.did(e, name, ins)
                steps.own()

            def row_sum(dst, src):
                return nc.vector.tensor_reduce(dst, src, AX_X, ALU.add)

            def begin(e):
                for who in "ap":
                    wait(dve, who, e, "begin")

            def norm_stats(e, tiles, v, when, part=""):
                for i, k in enumerate(tiles):
                    if i % QUARTER == 0:
                        yield next(when, None)
                    ins = nc.vector.bn_stats(stats[:, i, :], res[:, k, :])
                st = stats[:, 0:len(tiles), :]
                did(e, "stats" + part, ins)
                did(e, "diff" + part, nc.vector.tensor_tensor(v(0), st[:, :, 1], st[:, :, 4], ALU.subtract))
                did(e, "msum" + part, nc.vector.tensor_tensor(v(1), st[:, :, 1], st[:, :, 4], ALU.add))
                did(e, "vsum" + part, nc.vector.tensor_tensor(v(2), st[:, :, 2], st[:, :, 5], ALU.add))
                did(e, "dsq" + part, nc.vector.tensor_tensor(v(3), v(0), v(0), ALU.mult))
                did(e, "var" + part, nc.vector.scalar_tensor_tensor(v(4), v(3), P / 4.0, v(2), ALU.mult, ALU.add))
                did(e, "vareps" + part, nc.vector.tensor_scalar(v(5), v(4), 1.0 / P, LN_EPS, ALU.mult, ALU.add))
                yield next(when, None)
                wait(dve, "a", e, "std" + part)
                did(e, "rstd" + part, nc.vector.reciprocal(v(7), v(6)))
                did(e, "shift" + part, nc.vector.scalar_tensor_tensor(v(8), v(1), -0.5, v(7), ALU.mult, ALU.mult))
                if KINDS[e] == "rows":
                    half = e % 2
                    did(e, "rstd_d" + part, nc.vector.tensor_tensor(v(7), v(7), half_of(dinv, half), ALU.mult))
                    did(e, "shift_d" + part, nc.vector.tensor_tensor(v(8), v(8), half_of(dinv, half), ALU.mult))

            def artanh(e, pre, u, dst):
                did(e, pre + "plus", nc.vector.tensor_scalar(w(15), u, 1.0, None, ALU.add))
                did(e, pre + "minus", nc.vector.tensor_scalar(w(16), u, -1.0, 1.0, ALU.mult, ALU.add))
                did(e, pre + "inv", nc.vector.reciprocal(w(17), w(16)))
                did(e, pre + "ratio", nc.vector.tensor_tensor(w(18), w(15), w(17), ALU.mult))
                did(e, pre + "sq", nc.vector.tensor_tensor(w(20), u, u, ALU.mult))
                did(e, pre + "p1", nc.vector.tensor_scalar(w(21), w(20), 1.0 / 7, 1.0 / 5, ALU.mult, ALU.add))
                did(e, pre + "p2", nc.vector.tensor_tensor(w(21), w(21), w(20), ALU.mult))
                did(e, pre + "p3", nc.vector.scalar_tensor_tensor(w(21), w(21), 1.0 / 3, w(20), ALU.add, ALU.mult))
                did(e, pre + "p4", nc.vector.scalar_tensor_tensor(w(21), w(21), 1.0, u, ALU.add, ALU.mult))
                did(e, pre + "small", nc.vector.tensor_scalar(w(22), u, 0.1, None, ALU.is_lt))
                wait(dve, "a", e, pre + "ln")
                did(e, pre + "gap", nc.vector.scalar_tensor_tensor(w(23), w(19), -0.5, w(21), ALU.mult, ALU.add))
                did(e, pre + "pick", nc.vector.tensor_tensor(w(23), w(23), w(22), ALU.mult))
                did(e, pre + "artanh", nc.vector.scalar_tensor_tensor(dst, w(19), 0.5, w(23), ALU.mult, ALU.add))

            def lo_part(s, t, i=0):
                n, n_hi = lo_no[s, t], hi_no[s, t]
                dve.wait_ge(hi_ready, n_hi + 1 + BODY * i)
                slot_free(dve, s, t, i, n, lo_tile, LO)
                nc.vector.tensor_tensor(lo[:, n % LO, :], loaded(s, t), hi[:, n_hi % HI, :].bitcast(F32), ALU.subtract
                                        ).then_inc(lo_ready, 1)

            def bias_point():
                dve.wait_ge(setup_a, 2)
                nc.vector.tensor_scalar(bb[:, 2:3], bb[:, 1:2], MIN_NORM, None, ALU.max).then_inc(setup_v, 1)
                dve.wait_ge(setup_v, 1)
                nc.vector.reciprocal(bb[:, 4:5], bb[:, 2:3]).then_inc(setup_v, 1)
                dve.wait_ge(setup_v, 2)
                dve.wait_ge(setup_a, 3)
                nc.vector.scalar_tensor_tensor(bb[:, 5:6], bb[:, 3:4], MAX_NORM, bb[:, 4:5], ALU.min, ALU.mult).then_inc(setup_v, 1)
                dve.wait_ge(setup_v, 3)
                nc.vector.tensor_scalar(ball_bias[:], ball_bias[:], bb[:, 5:6], None, ALU.mult).then_inc(setup_v, 1)
                dve.wait_ge(setup_v, 4)
                dve.wait_ge(setup_a, 4)

            def enter():
                for h in range(2):
                    dve.wait_ge(x_in[h], 16)
                    for _ in norm_stats(0, range(h * HK, (h + 1) * HK), lambda i: half_of(w(i), h), iter(()), str(h)):
                        pass
                pad = [flat(half_of(operand[0], h)) for h in range(2)]
                for h in range(2):
                    for q, cols in enumerate(BANKS):
                        wait(dve, "p", 0, f"hT_{q}{h}")
                        did(0, f"hT_{q}{h}", nc.vector.tensor_copy(work[:, h, cols], acc(h)[:, cols]))
                    did(0, f"hh{h}", nc.vector.tensor_tensor(by_tile(pad[h]), half_of(rows, h), half_of(rows, h), ALU.mult))
                    did(0, f"hh_sum{h}", row_sum(half_of(w(9), h), by_tile(pad[h])))
                bias_point()
                for h in range(2):
                    wait(dve, "a", 0, f"mx_sq{h}")
                    did(0, f"mb{h}", nc.vector.tensor_tensor(by_tile(pad[h]), nat(h), per_feature(ball_bias), ALU.mult))
                    did(0, f"mb_sum{h}", row_sum(half_of(w(13), h), by_tile(pad[h])))
                wait(dve, "a", 0, "norms")
                did(0, "floor", nc.vector.tensor_scalar(sm[:, 11:13, :], sm[:, 11:13, :], MIN_NORM, None, ALU.max))
                did(0, "h_clip", nc.vector.tensor_scalar(w(14), w(11), CLIP, None, ALU.min))
                artanh_h = w(24)
                artanh(0, "h_", w(14), artanh_h)
                did(0, "hn_inv", nc.vector.reciprocal(w(25), w(11)))
                did(0, "arg", nc.vector.tensor_tensor(w(25), w(25), w(12), ALU.mult))
                did(0, "arg2", nc.vector.tensor_tensor(w(26), w(25), artanh_h, ALU.mult))
                wait(dve, "a", 0, "tanh")
                did(0, "cap", nc.vector.tensor_scalar(w(27), w(27), MAX_NORM, None, ALU.min))
                did(0, "mx_inv", nc.vector.reciprocal(w(28), w(12)))
                did(0, "q", nc.vector.tensor_tensor(w(28), w(27), w(28), ALU.mult))
                did(0, "q_sq", nc.vector.tensor_tensor(w(29), w(28), w(28), ALU.mult))
                did(0, "x2", nc.vector.tensor_tensor(w(29), w(29), w(10), ALU.mult))
                did(0, "xy", nc.vector.tensor_tensor(w(30), w(28), w(13), ALU.mult))
                did(0, "xy1", nc.vector.tensor_scalar(w(30), w(30), 2.0, 1.0, ALU.mult, ALU.add))
                did(0, "top", nc.vector.tensor_scalar(w(31), w(30), bb[:, 6:7], None, ALU.add))
                did(0, "left", nc.vector.tensor_scalar(w(32), w(29), -1.0, 1.0, ALU.mult, ALU.add))
                did(0, "x2y2", nc.vector.tensor_scalar(w(33), w(29), bb[:, 6:7], None, ALU.mult))
                did(0, "den", nc.vector.tensor_tensor(w(33), w(33), w(30), ALU.add))
                did(0, "den_floor", nc.vector.tensor_scalar(w(33), w(33), MIN_NORM, None, ALU.max))
                did(0, "den_inv", nc.vector.reciprocal(w(34), w(33)))
                did(0, "top_q", nc.vector.tensor_tensor(w(31), w(31), w(28), ALU.mult))
                did(0, "a", nc.vector.tensor_tensor(w(31), w(31), w(34), ALU.mult))
                did(0, "c", nc.vector.tensor_tensor(w(32), w(32), w(34), ALU.mult))
                did(0, "ax2", nc.vector.tensor_tensor(w(35), w(31), w(10), ALU.mult))
                did(0, "cxy", nc.vector.tensor_tensor(w(36), w(32), w(13), ALU.mult))
                did(0, "m_half", nc.vector.scalar_tensor_tensor(w(35), w(36), 2.0, w(35), ALU.mult, ALU.add))
                did(0, "m_part", nc.vector.tensor_tensor(w(35), w(35), w(31), ALU.mult))
                did(0, "cc", nc.vector.tensor_tensor(w(36), w(32), w(32), ALU.mult))
                did(0, "m_sum", nc.vector.scalar_tensor_tensor(w(9), w(36), bb[:, 6:7], w(35), ALU.mult, ALU.add))
                did(0, "m_guard", nc.vector.tensor_scalar(w(9), w(9), 0.0, None, ALU.max))
                lo_part(0, 0)
                wait(dve, "a", 0, "m_norm")
                did(0, "m_floor", nc.vector.tensor_scalar(w(11), w(11), MIN_NORM, None, ALU.max))
                did(0, "m_clip", nc.vector.tensor_scalar(w(14), w(11), MAX_NORM, None, ALU.min))
                artanh(0, "m_", w(14), w(24))
                did(0, "m_inv2", nc.vector.reciprocal(w(25), w(11)))
                did(0, "m_scale", nc.vector.tensor_tensor(w(25), w(25), w(24), ALU.mult))
                did(0, "a_out", nc.vector.tensor_tensor(w(31), w(31), w(25), ALU.mult))
                did(0, "c_out", nc.vector.tensor_tensor(w(32), w(32), w(25), ALU.mult))
                lo_part(0, 1)
                for h in range(2):
                    wait(dve, "a", 0, f"cb{h}")
                    for k in range(HK):
                        n_ = h * HK + k
                        ins = nc.vector.scalar_tensor_tensor(operand[0][:, n_, :], nat(h)[:, k, :], sm[:, 31, n_:n_ + 1],
                                                             by_tile(flat2(work))[:, n_, :], ALU.mult, ALU.add)
                    did(0, f"out{h}", ins)

            def add_rows(half, src, scale, when, ready=None, done=None):
                for k in range(HK):
                    if k % QUARTER == 0:
                        yield next(when)
                    if ready is not None and k % QUARTER == 0:
                        ready(k // QUARTER)
                    ins = nc.vector.scalar_tensor_tensor(res[:, half * HK + k, :], src[:, k, :], scale[:, k:k + 1],
                                                         res[:, half * HK + k, :], ALU.mult, ALU.add)
                    if done is not None and k % QUARTER == QUARTER - 1:
                        done(k // QUARTER, ins)
                return ins

            def inverse_sums(e, parts, total):
                did(e, "sum", nc.vector.tensor_tensor(total[:], parts[:, 0, :], parts[:, 1, :], ALU.add))
                did(e, "pos", nc.vector.tensor_scalar(pos[:], total[:], 0.0, None, ALU.is_gt))
                did(e, "masked", nc.vector.tensor_tensor(inv_sum[:], total[:], pos[:], ALU.mult))
                did(e, "one", nc.vector.tensor_scalar(one[:], pos[:], -1.0, 1.0, ALU.mult, ALU.add))
                did(e, "safe", nc.vector.tensor_tensor(inv_sum[:], inv_sum[:], one[:], ALU.add))
                did(e, "inv", nc.vector.reciprocal(inv_sum[:], inv_sum[:]))

            def epilogue(e):
                kind, half = KINDS[e], e % 2
                if kind == "none":
                    return
                when = iter(WHEN[kind, half]["v"])
                yield next(when)
                begin(e)
                if kind == "ball":
                    wait(dve, "a", e, "s_sq")
                    did(e, "s_sum", row_sum(v(9), by_tile(scr)))
                    yield next(when)
                    wait(dve, "a", e, "relu_sq")
                    did(e, "relu_sum", row_sum(v(10), nat(half)))
                    yield next(when)
                    wait(dve, "a", e, "norms")
                    did(e, "s_floor", nc.vector.tensor_scalar(v(13), v(11), MIN_NORM, None, ALU.max))
                    did(e, "s_inv", nc.vector.reciprocal(v(14), v(13)))
                    did(e, "s_scale", nc.vector.scalar_tensor_tensor(v(14), v(13), ARTANH_MAX_NORM, v(14), ALU.min, ALU.mult))
                    did(e, "u_norm", nc.vector.tensor_tensor(v(15), v(12), v(14), ALU.mult))
                    did(e, "u_floor", nc.vector.tensor_scalar(v(15), v(15), MIN_NORM, None, ALU.max))
                    did(e, "u_inv", nc.vector.reciprocal(v(17), v(15)))
                    yield next(when)
                    wait(dve, "a", e, "u_tanh")
                    did(e, "u_scale", nc.vector.scalar_tensor_tensor(v(18), v(16), MAX_NORM, v(17), ALU.min, ALU.mult))
                    did(e, "scale", nc.vector.tensor_tensor(v(18), v(18), v(14), ALU.mult))
                    did(e, "res", (yield from add_rows(half, by_tile(yT), v(18), when)))
                elif kind in ("swish", "swish_norm"):
                    wait(dve, "p", e, "nat3")
                    did(e, "biased", nc.vector.tensor_tensor(by_tile(scr), nat(half), per_feature(bias["swish"]), ALU.add))
                    if kind == "swish_norm":
                        yield next(when)
                        wait(dve, "a", e, "swish")
                        did(e, "res", nc.vector.tensor_tensor(half_of(res, half), half_of(res, half), by_tile(yT), ALU.add))
                elif kind == "columns":
                    wait(dve, "p", e, "nat3")
                    dve.wait_ge(hi_ready, hi_no[1, NK - 1] + 1)
                    inverse_sums(e, col_part, deg)
                    did(e, "res", (yield from add_rows(half, nat(half), half_of(inv_sum, half), when)))
                elif kind == "rows":
                    wait(dve, "p", e, "nat3")
                    dve.wait_ge(hi_ready, hi_no[7, NK - 1] + 1)
                    inverse_sums(e, row_part, deg)
                    yield next(when)
                    wait(dve, "a", e, "droot")
                    did(e, "dinv", nc.vector.reciprocal(dinv[:], droot[:]))
                    did(e, "res", (yield from add_rows(half, nat(half), half_of(inv_sum, half), when)))
                elif kind == "embed":
                    for k in range(HK):
                        q = k // QUARTER
                        if k % QUARTER == 0:
                            if q > 0:
                                yield next(when)
                            wait(dve, "p", e, f"nat{q}")
                        n_ = half * HK + k
                        ins = nc.vector.scalar_tensor_tensor(by_tile(scr)[:, k, :], nat(half)[:, k, :], dinv[:, n_:n_ + 1],
                                                             bias["embed"][:], ALU.mult, ALU.add)
                        if k % QUARTER == QUARTER - 1:
                            did(e, f"z{q}", ins)
                            part = by_tile(scr)[:, k + 1 - QUARTER:k + 1, :]
                            did(e, f"leaky{q}", nc.vector.scalar_tensor_tensor(
                                z[:, n_ + 1 - QUARTER:n_ + 1, :], part, 0.1, part, ALU.mult, ALU.max))
                elif kind == "last":
                    did(e, "biased", nc.vector.tensor_tensor(half_of(res, half), half_of(res, half),
                                                             per_feature(bias["last"]), ALU.add))
                    yield from add_rows(half, nat(half), half_of(dlast, half), when,
                                        lambda q: wait(dve, "p", e, f"nat{q}"),
                                        lambda q, ins: did(e, f"out{q}", ins))
                if kind in ("ball", "swish_norm", "rows"):
                    yield from norm_stats(e, range(half * HK, (half + 1) * HK), v, when)

            enter()

            def sum_near(k, i=0):
                if k == HK:
                    wait(dve, "p", NS, "near3")
                near = near_rows[:, k % GROUP, :, :]
                dve.wait_ge(near_scaled, k + 1 + GROUP * i)
                nc.vector.tensor_tensor(near[:, 0:2, :], near[:, 0:2, :], near[:, 2:4, :], ALU.add).then_inc(near_done, 1)
                dve.wait_ge(near_done, 2 * k + 1 + 2 * GROUP * i)
                nc.vector.tensor_tensor(near_sum[:, bass.ds(k % HK + GROUP * i, 1), :], near[:, 0:1, :], near[:, 1:2, :],
                                        ALU.add).then_inc(near_done, 1)

            for s, (mat, half, src, kind) in enumerate(SWEEPS):
                if s == LAST:
                    for _ in epilogue(s + 1):
                        pass
                    for h in range(2):
                        dve.wait_ge(za, ZA.index(f"sq{h}") + 1)
                        cols = slice(h * HALF, (h + 1) * HALF)
                        nc.vector.tensor_tensor(zT[:, 1, cols], acc(h), zT[:, 0, cols].bitcast(F32), ALU.subtract
                                                ).then_inc(zv, 1)
                    for h in range(2):
                        dve.wait_ge(za, ZA.index(f"row{h}") + 1)
                        row = sq_row[32:64, h * HALF:(h + 1) * HALF]
                        nc.vector.tensor_tensor(row, acc(h)[32:64, :], row.bitcast(F32), ALU.subtract).then_inc(zv, 1)

                    wait(dve, "a", s + 1, "z_sq")
                    nc.vector.tensor_scalar(neg_sq[:], z_sq[:], -1.0, None, ALU.mult).then_inc(zv, 1)
                    dve.wait_ge(zv, ZV.index("row1") + 1)
                    nc.vector.memset(acc(0), 0.0).then_inc(zv, 1)

                    def settle_a(g, i):
                        b, base = g % 2, len(GV) * g + 2 * len(GV) * i
                        dve.wait_ge(ranked, 2 * GROUP * (g + 1) + 4 * GROUP * i)
                        nc.vector.tensor_scalar(gd[:, b, :, :], top[:, b, :, 0:TOPK], 0.0, -1.0, ALU.min, ALU.mult).then_inc(gv, 1)
                        dve.wait_ge(gv, base + 1)
                        nc.vector.tensor_scalar(gd[:, b, :, :], gd[:, b, :, :], DIST_EPS, None, ALU.add).then_inc(gv, 1)

                    def settle_b(g, i):
                        b, base = g % 2, len(GV) * g + 2 * len(GV) * i
                        k = bass.ds(GROUP * g + 2 * GROUP * i, GROUP)
                        dve.wait_ge(ga, len(GA) * g + GA.index("weight") + 1 + 2 * len(GA) * i)
                        row_sum(gs[:, b, 0, :], near_w[:, k, :]).then_inc(gv, 1)
                        dve.wait_ge(gv, base + 3)
                        nc.vector.tensor_tensor(gs[:, b, 0, :], gs[:, b, 0, :], deg[:, k], ALU.add).then_inc(gv, 1)

                    def settle_c(g, i):
                        b, base = g % 2, len(GV) * g + 2 * len(GV) * i
                        k0 = GROUP * g + 2 * GROUP * i
                        k = bass.ds(k0, GROUP)
                        dve.wait_ge(ga, len(GA) * g + GA.index("root") + 1 + 2 * len(GA) * i)
                        nc.vector.reciprocal(dlast[:, k], gs[:, b, 1, :]).then_inc(gv, 1)
                        dve.wait_ge(gv, base + 5)
                        nc.vector.tensor_tensor(gs[:, b, 2, :], dlast[:, k], droot[:, k], ALU.mult).then_inc(gv, 1)
                        dve.wait_ge(gv, base + 6)
                        for r in range(GROUP):
                            tile = operand[0][:, bass.ds(k0 + r, 1), :]
                            ins = nc.vector.tensor_scalar(tile, tile, gs[:, b, 2, r:r + 1], None, ALU.mult)
                        ins.then_inc(gv, 1)
                        nc.vector.tensor_copy(near_at[:, k, :], top_at[:, b, :, 0:TOPK]).then_inc(gv, 1)

                    def rank(g, i=0):
                        for r in range(GROUP):
                            k = GROUP * g + r
                            dve.wait_ge(zz_out, 4 * (k + 1) + 8 * GROUP * i)
                            if g >= 2 and r == 0:
                                dve.wait_ge(gv, len(GV) * (g - 1) + 2 * len(GV) * i)
                            apart(dve)
                            nc.vector.max(top[:, g % 2, r, :], dist[k % 2][:, :]).then_inc(ranked, 1)
                            dve.wait_ge(ranked, 2 * k + 1 + 4 * GROUP * i)
                            apart(dve)
                            nc.vector.max_index(top_at[:, g % 2, r, :], top[:, g % 2, r, :], dist[k % 2][:, :]
                                                ).then_inc(ranked, 1)
                            if g > 0 and r == 1:
                                settle_b(g - 1, i)
                            if g > 0 and r == 3:
                                settle_c(g - 1, i)
                        settle_a(g, i)

                    rank(0)
                    rank(1)
                    with dve.Fori(0, NG // 2 - 1) as i:
                        rank(2, i)
                        rank(3, i)
                    settle_b(NG - 1, 0)
                    settle_c(NG - 1, 0)

                def split_group(g, i=0):
                    n = sx_no[s, g]
                    dve.wait_ge(sx_hi, n + 1 + (BODY // GROUP) * i)
                    nc.vector.tensor_tensor(split_x[:, n % 2, :, 1, :], operand[src][:, bass.ds(GROUP * g + BODY * i, GROUP), :],
                                            split_x[:, n % 2, :, 0, :].bitcast(F32), ALU.subtract).then_inc(sx_lo, 1)

                epi = Woven(None if s == LAST else epilogue(s + 1))
                for t in range(PEELED):
                    if (s, t // GROUP) in sx_no and t % GROUP == 0:
                        split_group(t // GROUP)
                    if (s, t) in lo_no and lo_no[s, t] >= AHEAD_LO:
                        lo_part(s, t)
                    if (s, t) in NEAR_AT:
                        sum_near(NEAR_AT[s, t])
                    epi.after(t)
                epi.finish()
                with dve.Fori(0, LOOPS) as i:
                    for t in range(PEELED, PEELED + BODY):
                        if t % GROUP == 0:
                            split_group(t // GROUP, i)
                        lo_part(s, t, i)
                        if (s, t) in NEAR_AT:
                            sum_near(NEAR_AT[s, t], i)
            for k in range(NK - NEAR_LEFT, NK):
                sum_near(k)
            for _ in epilogue(NS + 1):
                pass

        @block.gpsimd
        def _(pool):
            nc.gpsimd.memset(pick_half[:], -0.5).then_inc(setup_g, 1)
            nc.gpsimd.memset(two_rows[:].bitcast(F32), 0.0).then_inc(setup_g, 1)
            pool.wait_ge(setup_g, 2)
            nc.gpsimd.memset(two_rows[0:1, :].bitcast(F32), 1.0).then_inc(setup_g, 1)
            nc.gpsimd.memset(two_rows[32:33, :].bitcast(F32), 1.0).then_inc(setup_g, 1)

            def stage(g, i=0):
                if g >= 2:
                    pool.wait_ge(zz_done, 4 * GROUP * (g - 1) + 8 * GROUP * i)
                cols = bass.ds(GROUP * P * g + 2 * GROUP * P * i, GROUP * P)
                for part in range(2):
                    ins = nc.gpsimd.tensor_copy(split_x[:, g % 2, :, part, :], by_tile(zT[:, part, cols].bitcast(F32)))
                ins.then_inc(z_staged, 1)

            def stage_x(i):
                pool.wait_ge(gv, len(GV) + len(GV) * i)
                pool.wait_ge(tile_done, NK * LAST + RAW * i)
                nc.gpsimd.tensor_copy(early_x[:], operand[0][:, bass.ds(RAW * i, RAW), :]).then_inc(x_staged, 1)

            pool.wait_ge(setup_g, 4)
            pool.wait_ge(zv, 2)
            pool.wait_ge(tile_done, NK * LAST)
            stage(0)
            stage(1)
            with pool.Fori(0, NG // 2 - 1) as i:
                stage(2, i)
                stage_x(i)
                stage(3, i)

            for q in rows_out:
                pool.wait_ge(q, 16 * NG // 2)
            pool.wait_ge(gv, len(GV) * NG)
            for k in range(NK):
                if k >= GROUP:
                    pool.wait_ge(near_done, 2 * (k - GROUP + 1))
                for t in range(TOPK):
                    nc.gpsimd.indirect_dma_start(near_rows[:, k % GROUP, t, :], None, rows_dram,
                                                 bass.IndirectOffsetOnAxis(ap=near_at[:, k, t:t + 1], axis=0)
                                                 ).then_inc(fetched[k % GROUP], 16)

        @block.tensor
        def _(pe):
            steps = Steps(pe, "p")

            def epilogue(e):
                kind, half = KINDS[e], e % 2
                if kind == "none":
                    return
                when = iter(WHEN[kind, half]["p"])
                yield next(when)
                if kind == "last":
                    pe.wait_ge(near_done, 2 * HK * (half + 1))
                    for k in range(HK):
                        ins = nc.tensor.matmul(nat(half)[:, k, :], near_sum[:, k, :], weights["ident"][:],
                                               start=False, stop=True, skip_group_check=True)
                        if k % QUARTER == QUARTER - 1:
                            steps.did(e, f"near{k // QUARTER}", ins)
                    yield next(when)
                for k in range(HK):
                    if k % QUARTER == 0:
                        wait(pe, "a", e, f"yT{k // QUARTER}")
                    ins = nc.tensor.matmul(nat(half)[:, k, :], by_tile(yT)[:, k, :], weights[WEIGHT[kind]][:],
                                           start=True, stop=True, skip_group_check=True)
                    if k % QUARTER == QUARTER - 1:
                        steps.did(e, f"nat{k // QUARTER}", ins)

            pe.wait_ge(const_in, 16 * CONSTS)
            for h in range(2):
                for q in range(4):
                    wait(pe, "a", 0, f"h_{q}{h}")
                    for k in range(q * QUARTER, (q + 1) * QUARTER):
                        ins = nc.tensor.transpose(nat(h)[:, k, :], rows[:, h * HK + k, :], weights["ident"][:])
                    steps.did(0, f"hT_{q}{h}", ins)
                for q in range(4):
                    wait(pe, "v", 0, f"hT_{q}{h}")
                    for k in range(q * QUARTER, (q + 1) * QUARTER):
                        ins = nc.tensor.matmul(nat(h)[:, k, :], by_tile(work[:, h, :])[:, k, :], weights["ball"][:],
                                               start=True, stop=True)
                    steps.did(0, f"mx_{q}{h}", ins)

            for s, (mat, half, src, kind) in enumerate(SWEEPS):
                if s == LAST:
                    for h in range(2):
                        if h == 1:
                            for _ in epilogue(s + 1):
                                pass
                        for k in range(HK):
                            if h == 0 and k == 0:
                                wait(pe, "v", s, "leaky3")
                            if h == 1 and k % QUARTER == 0:
                                wait(pe, "v", s + 1, f"leaky{k // QUARTER}")
                            ins = nc.tensor.transpose(nat(h)[:, k, :], z[:, h * HK + k, :], weights["ident"][:])
                        ins.then_inc(zp, 1)
                    pe.wait_ge(setup_g, 4)
                    for h in range(2):
                        pe.wait_ge(za, ZA.index(f"sq{h}") + 1)
                        pe.wait_ge(zv, h + 1)
                        for b in range(4):
                            ins = nc.tensor.matmul(ps[:, 4 * h + b, :], pick_half[:], raw[:, h, b * BANK:(b + 1) * BANK],
                                                   start=True, stop=True)
                        ins.then_inc(zp, 1)
                    pe.wait_ge(zv, ZV.index("row1") + 1)
                    pe.wait_ge(za, len(ZA))

                    def early(j, i):
                        r = ring_no[s, j]
                        pe.wait_ge(x_staged, 1 + i)
                        pe.wait_ge(raw_in[r % RAW], 16 * (r // RAW + 1) + 16 * i)
                        for b in range(4):
                            ins = nc.tensor.matmul(ps[:, b, :], early_x[:, j, :], raw[:, r % RAW, b * BANK:(b + 1) * BANK],
                                                   start=False, stop=True, skip_group_check=True)
                        ins.then_inc(tile_done, 1)

                    def distances(g, i=0):
                        pe.wait_ge(z_staged, g + 1 + 2 * i)
                        for r in range(GROUP):
                            k = GROUP * g + r
                            for c in range(4):
                                n = 4 * k + c
                                if n >= 2:
                                    pe.wait_ge(zz_out, n - 1 + 8 * GROUP * i)
                                for b in (2 * c, 2 * c + 1):
                                    cols, bank = slice(b * BANK, (b + 1) * BANK), ps[:, 4 + b % 4, :]
                                    z_hi, z_lo = split_x[:, g % 2, r, 0, :], split_x[:, g % 2, r, 1, :]
                                    nc.tensor.matmul(bank, two_rows[:], sq_row[:, cols], start=True, stop=False)
                                    nc.tensor.matmul(bank, z_lo, zT[:, 0, cols], start=False, stop=False)
                                    nc.tensor.matmul(bank, z_hi, zT[:, 1, cols], start=False, stop=False)
                                    ins = nc.tensor.matmul(bank, z_hi, zT[:, 0, cols], start=False, stop=True)
                                ins.then_inc(zz_done, 1)
                            if g >= 2 and r % 2 == 1:
                                early(r // 2 + 2 * (g % 2), i)

                    distances(0)
                    distances(1)
                    pe.wait_ge(zv, ZV.index("zero") + 1)
                    with pe.Fori(0, NG // 2 - 1) as i:
                        distances(2, i)
                        distances(3, i)

                if s < 2:
                    wait(pe, "v", 0, f"out{s}")
                elif s > LAST:
                    pe.wait_ge(zz_out, 4 * NK)
                elif s < LAST:
                    who, name = PSUM_READ[KINDS[s]]
                    wait(pe, who, s, name)

                def products(t, i=0):
                    if t in WHOLE[s]:
                        wait_operand(pe, s, t // GROUP)
                        wait_tile(pe, s, t)
                        if s in SUMMED:
                            pe.wait_ge(hi_ready, hi_no[s, t] + 1)
                        parts = ((operand[src][:, t, :], loaded(s, t)),)
                    else:
                        n = sx_no[s, t // GROUP]
                        pe.wait_ge(sx_lo, n + 1 + (BODY // GROUP) * i)
                        pe.wait_ge(hi_ready, hi_no[s, t] + 1 + BODY * i)
                        pe.wait_ge(lo_ready, lo_no[s, t] + 1 + BODY * i)
                        x_hi, x_lo = split_x[:, n % 2, t % GROUP, 0, :], split_x[:, n % 2, t % GROUP, 1, :]
                        tile_hi, tile_lo = hi[:, hi_no[s, t] % HI, :], lo[:, lo_no[s, t] % LO, :]
                        parts = ((x_hi, tile_lo), (x_hi, tile_hi), (x_lo, tile_hi))
                    for j, (w, tile) in enumerate(parts):
                        for b in range(4):
                            ins = nc.tensor.matmul(ps[:, 4 * half + b, :], w, tile[:, b * BANK:(b + 1) * BANK],
                                                   start=(t == 0 and j == 0), stop=True, skip_group_check=True)
                    ins.then_inc(tile_done, 1)

                epi = Woven(None if s == LAST else epilogue(s + 1))
                for t in range(EARLY if s == LAST else 0, PEELED):
                    products(t)
                    epi.after(t)
                epi.finish()
                with pe.Fori(0, LOOPS) as i:
                    for t in range(PEELED, PEELED + BODY):
                        products(t, i)
            for _ in epilogue(NS + 1):
                pass


def kernel(x, adj, L0_gnn_weight, L0_gnn_bias, L1_gnn_W, L1_gnn_b, L2_gnn_W_in, L2_gnn_W_out,
           L3_gnn_W1, L3_gnn_b1, L3_gnn_W2, L3_gnn_b2):
    import concourse.bacc as bacc
    from concourse.bass_utils import run_bass_kernel_spmd

    arrays = {
        "x": x, "adj": adj, "adj_t": np.asarray(adj).T, "w_ball_t": np.asarray(L0_gnn_weight).T,
        "b_ball": L0_gnn_bias, "w_swish": L1_gnn_W, "b_swish": L1_gnn_b, "w_in": L2_gnn_W_in,
        "w_out": L2_gnn_W_out, "w_embed": L3_gnn_W1, "b_embed": L3_gnn_b1, "w_last": L3_gnn_W2,
        "b_last": L3_gnn_b2, "eye": np.eye(P, dtype=np.float32)}
    arrays = {n: np.ascontiguousarray(a) for n, a in arrays.items()}
    nc = bacc.Bacc("TRN2", target_bir_lowering=False, num_devices=1)
    args = [nc.dram_tensor(n, a.shape, F32, kind="ExternalInput").ap() for n, a in arrays.items()]
    rows_dram = nc.dram_tensor("rows", (N, P), F32, kind="Internal").ap()
    out = nc.dram_tensor("out", (N, P), F32, kind="ExternalOutput").ap()
    graph_layers(nc, *args, rows_dram, out)
    r = run_bass_kernel_spmd(nc, [arrays], core_ids=[0])
    return r.results[0]["out"]
```
